# Optimizing a Trainium2 kernel written in Bass

```python
import numpy as np
import jax
import jax.numpy as jnp

def _softmax(x, axis=-1):
    return jax.nn.softmax(x, axis=axis)

def _gelu(x):
    return jax.nn.gelu(x, approximate=True)

def _silu(x):
    return jax.nn.silu(x)

def _sigmoid(x):
    return jax.nn.sigmoid(x)

def _layernorm(x, axis=-1, eps=1e-05):
    m = jnp.mean(x, axis=axis, keepdims=True)
    v = jnp.var(x, axis=axis, keepdims=True)
    return (x - m) / jnp.sqrt(v + eps)

def _scatter_add(tgt, idx, src, axis=0):
    return tgt.at[idx].add(src)

def _segment_sum(src, seg, n):
    return jax.ops.segment_sum(src, seg, n)
kernel_name = 'mk_seq_preln_d1_jaxref_r4_46033b'

def setup_inputs(seed: int=0):
    np.random.seed(seed)
    _w = jnp.asarray

    def _L0_attn_setup():
        import jax, jax.numpy as jnp
        import numpy as np
        D = 512
        H = 16
        HD = D // H
        key = jax.random.key(seed)
        k1, k2, k3 = jax.random.split(key, 3)
        x = jax.random.normal(k1, (2, 512, D), dtype=jnp.float32)
        Wqkv = jax.random.normal(k2, (D, 3 * D), dtype=jnp.float32) * D ** (-0.5)
        Wo = jax.random.normal(k3, (D, D), dtype=jnp.float32) * D ** (-0.5)
        return {'x': x, 'Wqkv': Wqkv, 'Wo': Wo}
    _L0_attn_in = _L0_attn_setup()

    def _L0_ffn_setup():
        import jax, jax.numpy as jnp
        import numpy as np
        D_MODEL = 512
        HIDDEN = int(2 * D_MODEL * 4 / 3)

        def ternary_quant(w):
            s = jnp.mean(jnp.abs(w))
            q = jnp.clip(jnp.round(w / s), -1.0, 1.0) * s
            return w + jax.lax.stop_gradient(q - w)
        key = jax.random.key(seed)
        k0, k1, k2, k3 = jax.random.split(key, 4)
        x = jax.random.normal(k0, (4, 1024, D_MODEL), dtype=jnp.float32)
        std_in = 1.0 / np.sqrt(D_MODEL)
        std_h = 1.0 / np.sqrt(HIDDEN)
        w1 = jax.random.uniform(k1, (HIDDEN, D_MODEL), jnp.float32, -std_in, std_in)
        w3 = jax.random.uniform(k2, (HIDDEN, D_MODEL), jnp.float32, -std_in, std_in)
        w2 = jax.random.uniform(k3, (D_MODEL, HIDDEN), jnp.float32, -std_h, std_h)
        return {'x': x, 'w1': w1, 'w3': w3, 'w2': w2}
    _L0_ffn_in = _L0_ffn_setup()
    _d = {'L0_attn_x': _L0_attn_in['x'], 'L0_attn_Wqkv': _L0_attn_in['Wqkv'], 'L0_attn_Wo': _L0_attn_in['Wo'], 'L0_ffn_w1': _L0_ffn_in['w1'], 'L0_ffn_w3': _L0_ffn_in['w3'], 'L0_ffn_w2': _L0_ffn_in['w2']}
    _x0 = _d['L0_attn_x']
    _d['L0_attn_x'] = jax.random.normal(jax.random.fold_in(jax.random.key(seed), 1), (4, 512, 512), dtype=_x0.dtype)
    del _x0
    return _d

def reference(L0_attn_x, L0_attn_Wqkv, L0_attn_Wo, L0_ffn_w1, L0_ffn_w3, L0_ffn_w2):

    def _L0_attn_ref(x, Wqkv, Wo):
        import jax, jax.numpy as jnp
        import numpy as np
        D = 512
        H = 16
        HD = D // H
        B, S, _ = x.shape
        qkv = (x @ Wqkv).reshape(B, S, 3, H, HD)
        q = qkv[:, :, 0].transpose(0, 2, 1, 3)
        k = qkv[:, :, 1].transpose(0, 2, 1, 3)
        v = qkv[:, :, 2].transpose(0, 2, 1, 3)
        scores = jnp.einsum('bhqd,bhkd->bhqk', q, k) * HD ** (-0.5)
        causal = jnp.tril(jnp.ones((S, S), dtype=bool))
        scores = jnp.where(causal, scores, jnp.float32(-1000000000.0))
        a = jax.nn.softmax(scores, axis=-1)
        o = jnp.einsum('bhqk,bhkd->bhqd', a, v)
        o = o.transpose(0, 2, 1, 3).reshape(B, S, H * HD)
        return o @ Wo

    def _L0_ffn_ref(x, w1, w3, w2):
        import jax, jax.numpy as jnp
        import numpy as np
        D_MODEL = 512
        HIDDEN = int(2 * D_MODEL * 4 / 3)

        def ternary_quant(w):
            s = jnp.mean(jnp.abs(w))
            q = jnp.clip(jnp.round(w / s), -1.0, 1.0) * s
            return w + jax.lax.stop_gradient(q - w)
        w1q = ternary_quant(w1)
        w3q = ternary_quant(w3)
        w2q = ternary_quant(w2)
        h1 = jnp.einsum('bsd,hd->bsh', x, w1q)
        h3 = jnp.einsum('bsd,hd->bsh', x, w3q)
        g = jax.nn.silu(h1) * h3
        return jnp.einsum('bsh,dh->bsd', g, w2q)
    x = L0_attn_x
    x = x + _L0_attn_ref(_layernorm(x, axis=-1), L0_attn_Wqkv, L0_attn_Wo)
    x = x + _L0_ffn_ref(_layernorm(x, axis=-1), L0_ffn_w1, L0_ffn_w3, L0_ffn_w2)
    return x

_drawn_inputs = setup_inputs


def setup_inputs(seed=0):
    import zlib

    import numpy as np

    out = dict(_drawn_inputs(seed))
    spreads = {}
    factors = {}
    for name, (base, spread) in spreads.items():
        noise = np.random.default_rng([zlib.crc32(name.encode()), seed]).standard_normal(out[name].shape)
        drawn = base * np.exp(spread * noise) if base else spread * noise
        out[name] = jnp.asarray(drawn.astype(out[name].dtype))
    for name, factor in factors.items():
        out[name] = (out[name] * factor).astype(out[name].dtype)
    return out
```

```python
from contextlib import ExitStack
import math

import concourse.bass as bass
from concourse import mybir

F32 = mybir.dt.float32
F16 = mybir.dt.float16
ACT = mybir.ActivationFunctionType
ALU = mybir.AluOpType
AX_X = mybir.AxisListType.X
RMAX = bass.bass_isa.ReduceOp.max
RADD = bass.bass_isa.ReduceOp.add

P = 128
D = 512
S = 512
BATCHES = 4
HD = 32
HEADS = D // HD
HG = P // HD
GROUPS = HEADS // HG
KC = D // P
ST = S // P
HIDDEN = int(2 * D * 4 / 3)
HC = -(-HIDDEN // P)
HLAST = HIDDEN - (HC - 1) * P
EPS = 1e-5

NORM_SCALE = 16.0
WEIGHT_TOP = 64.0
QK_SHRINK = 1.0 / 128
V_SHRINK = 1.0 / 16
MAX_UNIT = 32768.0
MASK = 60000.0
G_SHRINK = 1.0 / 4096

UNITS = []
for pair in range(HG // 2):
    h = 2 * pair
    UNITS += [[(h, 3, 0, 512)], [(h, 2, 0, 384), (h, 0, 384, 128)],
              [(h, 1, 0, 256), (h + 1, 1, 256, 256)],
              [(h + 1, 3, 0, 512)], [(h + 1, 2, 0, 384), (h + 1, 0, 384, 128)]]
NU = len(UNITS)
PIECES = NU // 2
STACK_DMAS = HG * 6
SELECTS = 6

WEIGHTS = ("w1", "w3", "w2")


def order(attend, feed, prefetch, prepare):
    o = []
    fillers = []
    if feed:
        for c in range(HC):
            fillers += [("gate", c), ("lin", c)]
    if prepare:
        fillers += [("weight_load", "w1"), None, ("weight_sum", "w1"), None]
        for m, after in zip(WEIGHTS, WEIGHTS[1:] + (None,)):
            fillers += [("weight_ternary", m), None]
            if after:
                fillers.append(("weight_load", after))
            fillers += [("weight_turn", m, c) for c in range(HC)]
            if after:
                fillers += [("weight_sum", after), None]
    rate = 2 if prepare else 1

    def fill(k):
        for _ in range(k * rate):
            if fillers:
                step = fillers.pop(0)
                if step:
                    o.append(step)

    if not attend:
        o += [("yt", i) for i in range(ST)]
        fill(len(fillers))
        return o + [("down", i) for i in range(ST)]
    o += [("xt", i) for i in range(ST)]
    o += [("q", 0), ("k", 0), ("v", 0), ("v", 1)]
    if prefetch:
        o.append(("x_load",))
    if prepare:
        o.append(("wo_split",))
    if feed:
        o += [("yt", i) for i in range(ST)]
    fill(2)
    for p in range(PIECES):
        o.append(("scores", 0, p))
        if p < 2:
            o.append(("v", p + 2))
        elif p < 5:
            fill(1)
    o += [("q", 1), ("k", 1), ("max_row", 0)]
    fill(2)
    for g in range(GROUPS - 1):
        for p in range(PIECES):
            o += [("scores", g + 1, p), ("probs", g, p)]
            if p == 2:
                fill(1)
        if g + 2 < GROUPS:
            o += [("q", g + 2), ("k", g + 2)]
        else:
            fill(2)
        o += [("max_row", g + 1), ("values", g)]
        if g == 1 and prefetch:
            o.append(("norm_x",))
        fill(2)
    for p in range(PIECES):
        o.append(("probs", GROUPS - 1, p))
        if p < PIECES - 1:
            fill(1)
    fill(len(fillers))
    if feed:
        o += [("down", 0), ("down", 1)]
    o.append(("values", GROUPS - 1))
    if feed:
        o += [("down", 2), ("down", 3)]
    o += [("project", i) for i in range(ST)]
    o.append(("norm_y",))
    return o


HALF_STEPS = ("xt", "yt", "q", "k", "max_row")
WORK_STEPS = ("xt", "yt", "q", "k", "v", "max_row", "project", "gate", "lin", "down", "weight_turn")


def numbered(steps, kinds):
    found = [s for s in steps if s[0] in kinds]
    return {s: n for n, s in enumerate(found)}


FIRST = order(True, False, True, True)
MIDDLE = order(True, True, True, False)
LAST_ATTENTION = order(True, True, False, False)
LAST = order(False, True, False, False)


class Pass:

    def __init__(self, steps, att, ffn, before=(), rounds=0):
        self.steps, self.att, self.ffn, self.rounds = steps, att, ffn, rounds
        self.first = steps is FIRST
        self.uses, self.halves = numbered(steps, WORK_STEPS), numbered(steps, HALF_STEPS)
        self.uses_before = sum(len(numbered(s, WORK_STEPS)) for s in before)
        self.halves_before = sum(len(numbered(s, HALF_STEPS)) for s in before)

    def slot(self, step):
        return (self.uses_before + self.uses[step]) % 2

    def use(self, step):
        k = (self.uses_before + self.uses[step]) // 2 + 1
        return k if isinstance(self.rounds, int) and self.rounds == 0 else self.rounds * (MIDDLE_USES // 2) + k

    def half(self, step):
        k = self.halves_before + self.halves[step] + 1
        return k if isinstance(self.rounds, int) and self.rounds == 0 else self.rounds * MIDDLE_HALVES + k


MIDDLE_USES = len(numbered(MIDDLE, WORK_STEPS))
MIDDLE_HALVES = len(numbered(MIDDLE, HALF_STEPS))
assert MIDDLE_USES % 2 == 0


def passes(engine, run):
    run(Pass(FIRST, 0, None))
    with engine.Fori(1, BATCHES - 1) as t:
        run(Pass(MIDDLE, t, t - 1, [FIRST], t - 1))
    before = [FIRST] + [MIDDLE] * (BATCHES - 2)
    run(Pass(LAST_ATTENTION, BATCHES - 1, BATCHES - 2, before))
    run(Pass(LAST, None, BATCHES - 1, before + [LAST_ATTENTION]))


def build(nc, x, wqkv, wo, w1, w3, w2, out):
    x_v = x.rearrange("b (i p) d -> b p i d", p=P)
    out_v = out.rearrange("b (i p) d -> b p i d", p=P)
    wqkv_v = wqkv.rearrange("(c p) n -> p c n", p=P)
    wo_v = wo.rearrange("(c p) n -> p c n", p=P)
    w_dram = {"w1": w1, "w3": w3, "w2": w2}

    with ExitStack() as ctx:
        def sb(name, shape, dt):
            return ctx.enter_context(nc.sbuf_tensor(name, shape, dt))

        def psum(name, shape, dt):
            return ctx.enter_context(nc.psum_tensor(name, shape, dt))

        def sem(name):
            return ctx.enter_context(nc.semaphore(name))

        wqkv_hi = sb("wqkv_hi", [P, KC, 3 * D], F16)
        wqkv_lo = sb("wqkv_lo", [P, KC, 3 * D], F16)
        wo_hi = sb("wo_hi", [P, KC, D], F16)
        wo_lo = sb("wo_lo", [P, KC, D], F16)
        t_up = {m: sb(f"{m}_ternary", [P, KC, HIDDEN], F16) for m in ("w1", "w3")}
        t_down = sb("w2_ternary", [P, HC, D], F16)
        ident = sb("ident", [P, P], F32)
        ident16 = sb("ident16", [P, P], F16)
        mask_rows = sb("mask_rows", [P, P], F16)
        mask_cols = sb("mask_cols", [P, P], F16)
        ones = sb("ones", [P, HD], F32)
        neg_half = sb("neg_half", [P, ST], F32)
        scalars = sb("scalars", [P, 32], F32)
        xn = sb("xn", [P, ST, D], F32)
        x_res = sb("x_res", [P, ST, D], F32)
        xt_hi = sb("xt_hi", [P, KC, S], F16)
        xt_lo = sb("xt_lo", [P, KC, S], F16)
        v_sb = sb("v_sb", [P, ST, D], F32)
        halves = [{n: sb(f"{n}_{i}", [P, S], F16) for n in ("q_hi", "q_lo", "k_hi", "k_lo")} for i in range(2)]
        q_stack = [sb(f"q_stack{i}", [P, HG, S], F16) for i in range(2)]
        k_stack = [sb(f"k_stack{i}", [P, HG, S], F16) for i in range(2)]
        block_max = sb("block_max", [P, NU, 4], F32)
        neg_max = sb("neg_max", [P, HG, ST], F32)
        max_hi = sb("max_hi", [HG * ST, P], F16)
        max_lo = sb("max_lo", [HG * ST, P], F16)
        probs = sb("probs", [P, NU, 512], F32)
        inv_sum = sb("inv_sum", [P, S], F32)
        o_sb = sb("o_sb", [P, S], F32)
        ot_hi = sb("ot_hi", [P, GROUPS, S], F16)
        ot_lo = sb("ot_lo", [P, GROUPS, S], F16)
        stats = {n: sb(f"{n}_stats", [P, ST, 6], F32) for n in "xy"}
        mean_var = {n: sb(f"{n}_mean_var", [P, ST, 2], F32) for n in "xy"}
        var_eps = {n: sb(f"{n}_var_eps", [P, ST], F32) for n in "xy"}
        rstd = {n: sb(f"{n}_rstd", [P, ST], F32) for n in "xy"}
        RAW = HC * D
        late = sb("late", [P, 36864 // 4], F32)
        g_hi = late[:, 0:HC * S // 2].bitcast(F16).rearrange("p (c s) -> p c s", c=HC)
        g_lo = late[:, HC * S // 2:HC * S].bitcast(F16).rearrange("p (c s) -> p c s", c=HC)
        yt_hi = late[:, RAW:RAW + 1024].bitcast(F16).rearrange("p (c s) -> p c s", c=KC)
        yt_lo = late[:, RAW + 1024:RAW + 2048].bitcast(F16).rearrange("p (c s) -> p c s", c=KC)
        sig = late[:, RAW + 2048:RAW + 2560]
        g32 = [late[:, RAW + 2560:RAW + 3072], late[:, RAW + 3072:RAW + 3584]]
        yn = sb("yn", [P, ST, D], F32)
        wqkv_raw = late[:, 0:KC * 3 * D].rearrange("p (c n) -> p c n", c=KC)
        wo_raw = late[:, KC * 3 * D:KC * 4 * D].rearrange("p (c n) -> p c n", c=KC)
        raw_rows = late[:, 0:HC * D].rearrange("p (c n) -> p c n", c=HC)
        raw_down = late[:, 0:ST * HIDDEN].rearrange("p (c n) -> p c n", c=ST)
        raw = {"w1": late[:, 0:HC * D], "w3": late[:, 0:HC * D], "w2": late[:, 0:ST * HIDDEN]}
        raw_n = {"w1": HC * D, "w3": HC * D, "w2": ST * HIDDEN}
        nat = late[:, HC * D:HC * D + HC * D // 2].bitcast(F16)
        below = yn[:].rearrange("p i d -> p (i d)").bitcast(F16)
        BELOW = 2 * ST * D

        TERNARY_PARTS = -(-RAW // BELOW)

        def scalar(i, n=1):
            return scalars[:, i:i + n]
        wmax_part, wmax_all, w_scale, wo_part, womax_all, wo_scale = 0, 4, 5, 6, 7, 8
        exp_scale, project_scale, down_scale, tanh_scale, tmp = 9, 10, 11, 12, 13
        abs_sum = {"w1": 14, "w3": 15, "w2": 16}
        abs_all = {"w1": 17, "w3": 18, "w2": 19}
        half_s = {"w1": 20, "w3": 21, "w2": 22}
        neg_half_s = {"w1": 23, "w3": 24, "w2": 25}

        work = [psum(f"work{i}", [P, 512], F32) for i in range(2)]
        score_bank = [psum(f"score_bank{i}", [P, 512], F32) for i in range(2)]
        prob_bank = [psum(f"prob_bank{i}", [P, 512], F32) for i in range(2)]
        o_bank = psum("o_bank", [P, S], F32)
        sum_bank = psum("sum_bank", [P, S], F32)

        x_loaded = sem("x_loaded")
        res_loaded = [sem(f"res_loaded{i}") for i in range(ST)]
        wqkv_loaded = [sem(f"wqkv_loaded{i}") for i in range(KC)]
        wo_loaded = sem("wo_loaded")
        raw_loaded = sem("raw_loaded")
        out_stored = [sem(f"out_stored{i}") for i in range(ST)]
        stacked = [sem(f"stacked{i}") for i in range(2)]
        max_placed = [sem(f"max_placed{i}") for i in range(2)]
        stats_done = {n: sem(f"{n}_stats_done") for n in "xy"}
        aggr_done = {n: sem(f"{n}_aggr_done") for n in "xy"}
        var_done = {n: sem(f"{n}_var_done") for n in "xy"}
        rstd_done = {n: sem(f"{n}_rstd_done") for n in "xy"}
        norm_done = {n: sem(f"{n}_norm_done") for n in "xy"}
        work_full = [sem(f"work_full{i}") for i in range(2)]
        work_free = [sem(f"work_free{i}") for i in range(2)]
        work_half = sem("work_half")
        score_full = sem("score_full")
        score_free = sem("score_free")
        max_ready = sem("max_ready")
        prob_full = sem("prob_full")
        prob_free = sem("prob_free")
        selected = sem("selected")
        values_full = sem("values_full")
        inv_done = sem("inv_done")
        o_ready = sem("o_ready")
        o_hi_done = sem("o_hi_done")
        o_lo_done = sem("o_lo_done")
        tanh_done = sem("tanh_done")
        g_hi_done = sem("g_hi_done")
        g_lo_done = sem("g_lo_done")
        sp_passed, pool_passed, dve_passed = (sem(n) for n in ("sp_passed", "pool_passed", "dve_passed"))
        zeroed = sem("zeroed")
        consts_done = sem("consts_done")
        mask_scaled = sem("mask_scaled")
        part_max_done = sem("part_max_done")
        wmax_done = sem("wmax_done")
        reduced = sem("reduced")
        setup = sem("setup")
        weights_hi = sem("weights_hi")
        weights_split = sem("weights_split")
        pad_zeroed = sem("pad_zeroed")
        abs_summed = sem("abs_summed")
        below_done = sem("below_done")
        ternary_done = sem("ternary_done")
        turned = sem("turned")

        def count(b, per, k):
            return b * per + k

        block = ctx.enter_context(nc.Block())

        @block.sync
        def _(sp):
            def wait(semaphore, value):
                sp.wait_ge(semaphore, value)
                sp.sem_inc(sp_passed, 1)

            sp.dma_start(xn[:], x_v[0]).then_inc(x_loaded, 16)
            for c in range(KC):
                sp.dma_start(wqkv_raw[:, c, :], wqkv_v[:, c, :]).then_inc(wqkv_loaded[c], 16)
            sp.dma_start(wo_raw, wo_v).then_inc(wo_loaded, 16)
            for i in range(ST):
                sp.dma_start(x_res[:, i, :], x_v[0, :, i, :]).then_inc(res_loaded[i], 16)

            def x_load(ps):
                wait(work_full[ps.slot(("q", 0))], ps.use(("q", 0)))
                sp.dma_start(xn[:], x_v[ps.att + 1]).then_inc(x_loaded, 16)

            def stack(ps, g):
                i, half = g % 2, halves[g % 2]
                for use in (("q", g), ("k", g)):
                    wait(work_free[ps.slot(use)], ps.use(use))
                if g >= 2 or not ps.first:
                    wait(prob_full, count(ps.att, NU * GROUPS, NU * (g - 1)))
                for h in range(HG):
                    rows = slice(HD * h, HD * (h + 1))
                    for dst, names in ((q_stack[i], ("q_hi", "q_lo", "q_hi")), (k_stack[i], ("k_hi", "k_hi", "k_lo"))):
                        for j, n in enumerate(names):
                            sp.dma_start(dst[HD * j:HD * (j + 1), h, :], half[n][rows, :]).then_inc(stacked[i], 16)

            def max_row(ps, g):
                use = ("max_row", g)
                wait(work_free[ps.slot(use)], ps.use(use))
                for j, src in enumerate((max_hi, max_lo)):
                    dst = q_stack[g % 2][3 * HD + j:3 * HD + j + 1, :, :].rearrange("o h (t q) -> o (h t) q", q=P)
                    sp.dma_start(dst, src[:]).then_inc(max_placed[g % 2], 16)

            def down(ps, i):
                use = ("down", i)
                wait(work_free[ps.slot(use)], ps.use(use))
                sp.dma_start(out_v[ps.ffn, :, i, :], x_res[:, i, :]).then_inc(out_stored[i], 16)
                if ps.att is not None:
                    wait(out_stored[i], count(ps.ffn, 16, 16))
                    sp.dma_start(x_res[:, i, :], x_v[ps.att, :, i, :]).then_inc(res_loaded[i], 16)

            def weight_load(m):
                n = WEIGHTS.index(m)
                if n == 0:
                    sp.wait_ge(weights_split, KC + 1)
                    sp.wait_ge(pad_zeroed, 1)
                else:
                    sp.wait_ge(ternary_done, TERNARY_PARTS * n)
                if m == "w2":
                    sp.dma_start(raw_down, w2.rearrange("(c p) n -> p c n", p=P)).then_inc(raw_loaded, 16)
                else:
                    sp.dma_start(raw_rows[:, 0:HC - 1, :],
                                 w_dram[m][0:(HC - 1) * P, :].rearrange("(c p) n -> p c n", p=P)).then_inc(raw_loaded, 16)
                    sp.dma_start(raw_rows[0:HLAST, HC - 1, :], w_dram[m][(HC - 1) * P:HIDDEN, :]).then_inc(raw_loaded, 16)

            def run(ps):
                for step in ps.steps:
                    if step[0] == "x_load":
                        x_load(ps)
                    elif step[0] == "k":
                        stack(ps, step[1])
                    elif step[0] == "max_row":
                        max_row(ps, step[1])
                    elif step[0] == "down":
                        down(ps, step[1])
                    elif step[0] == "weight_load":
                        weight_load(step[1])

            passes(sp, run)
            for i in range(ST):
                sp.wait_ge(out_stored[i], 16 * BATCHES)

        @block.gpsimd
        def _(pool):
            pool.memset(ident[:], 0.0).then_inc(zeroed, 1)
            pool.memset(ident16[:], 0.0).then_inc(zeroed, 1)
            pool.memset(mask_cols[:], 0.0).then_inc(zeroed, 1)
            pool.memset(ones[:], 1.0).then_inc(consts_done, 1)
            pool.memset(neg_half[:], -0.5).then_inc(consts_done, 1)
            pool.wait_ge(zeroed, 3)
            for t in (ident, ident16):
                pool.affine_select(out=t[:], in_=t[:], compare_op=ALU.not_equal, fill=1.0, base=0,
                                   pattern=[[-1, P]], channel_multiplier=1).then_inc(consts_done, 1)
            pool.affine_select(out=mask_cols[:], in_=mask_cols[:], compare_op=ALU.is_ge, fill=MASK, base=0,
                               pattern=[[-1, P]], channel_multiplier=1).then_inc(consts_done, 1)

            def power(n, b):
                pool.wait_ge(var_done[n], count(b, 1, 1))
                pool.tensor_tensor(rstd[n][:], var_eps[n][:], neg_half[:], ALU.pow).then_inc(rstd_done[n], 1)

            def all_reduce(dst, src, op):
                pool.partition_all_reduce(scalar(dst), scalar(src), P, op).then_inc(reduced, 1)

            pool.wait_ge(consts_done, 7)
            power("x", 0)
            pool.wait_ge(wmax_done, 1)
            all_reduce(wmax_all, wmax_all, RMAX)
            pool.wait_ge(wmax_done, 2)
            all_reduce(womax_all, womax_all, RMAX)

            def select(ps, g, p):
                pairs = {2: 0, 4: 1}
                if p not in pairs:
                    return
                u = 5 * pairs[p]
                pool.wait_ge(prob_free, count(ps.att, NU * GROUPS, NU * g + u + 5))
                pool.sem_inc(pool_passed, 1)
                blocks = probs[:, u:u + 5, :].rearrange("p u (k c) -> p (u k) c", c=P)
                for first, step_, n in ((0, 4, 5), (7, 3, 2), (19, 1, 1)):
                    view = blocks[:, first:first + step_ * (n - 1) + 1:step_, :]
                    pool.affine_select(out=view, in_=view, compare_op=ALU.is_ge, fill=0.0, base=0,
                                       pattern=[[0, n], [1, P]], channel_multiplier=-1).then_inc(selected, 1)

            def values(ps, g):
                pool.wait_ge(o_hi_done, count(ps.att, GROUPS, g + 1))
                pool.tensor_tensor(ot_lo[:, g, :], o_sb[:], ot_hi[:, g, :], ALU.subtract).then_inc(o_lo_done, 1)

            def lin(ps, c):
                m = P if c < HC - 1 else HLAST
                pool.wait_ge(g_hi_done, count(ps.ffn, HC, c + 1))
                pool.tensor_tensor(g_lo[0:m, c, :], g32[c % 2][0:m, :], g_hi[0:m, c, :],
                                   ALU.subtract).then_inc(g_lo_done, 1)

            def weight_sum(m):
                n = WEIGHTS.index(m)
                pool.wait_ge(abs_summed, n + 1)
                all_reduce(abs_all[m], abs_sum[m], RADD)

            def run(ps):
                for step in ps.steps:
                    if step[0] == "probs":
                        select(ps, step[1], step[2])
                    elif step[0] == "values":
                        values(ps, step[1])
                    elif step[0] == "lin":
                        lin(ps, step[1])
                    elif step[0] == "norm_x":
                        power("x", ps.att + 1)
                    elif step[0] == "norm_y":
                        power("y", ps.att)
                    elif step[0] == "weight_sum":
                        weight_sum(step[1])

            passes(pool, run)

        @block.scalar
        def _(act):
            for c in range(KC):
                if c == 0:
                    act.wait_ge(setup, 2)
                act.activation(wqkv_hi[:, c, :], wqkv_raw[:, c, :], ACT.Copy,
                               scale=scalar(w_scale)).then_inc(weights_hi, 1)
            def turned_high(ps, step, dst, i):
                s = ps.slot(step)
                act.wait_ge(work_full[s], ps.use(step))
                act.activation(dst[:, :, i * P:(i + 1) * P], work[s][:].rearrange("p (c s) -> p c s", c=KC),
                               ACT.Copy).then_inc(work_half, 1)

            def qk(ps, step):
                g = step[1]
                s, name = ps.slot(step), step[0] + "_hi"
                if step[0] == "q" and (g >= 2 or not ps.first):
                    act.wait_ge(stacked[g % 2], count(ps.att, 32 * STACK_DMAS, 16 * STACK_DMAS * (g // 2)))
                act.wait_ge(work_full[s], ps.use(step))
                act.activation(halves[g % 2][name][:], work[s][:], ACT.Copy, scale=QK_SHRINK).then_inc(work_half, 1)

            def v(ps, step):
                i, s = step[1], ps.slot(step)
                act.wait_ge(work_full[s], ps.use(step))
                act.activation(v_sb[:, i, :], work[s][:], ACT.Copy, scale=V_SHRINK).then_inc(work_free[s], 1)

            def max_row(ps, step):
                s = ps.slot(step)
                act.wait_ge(work_full[s], ps.use(step))
                act.activation(max_hi[:], work[s][0:HG * ST, 0:P], ACT.Copy,
                               scale=1.0 / MAX_UNIT).then_inc(work_half, 1)

            def exp(ps, g, p):
                for u in (2 * p, 2 * p + 1):
                    act.wait_ge(prob_full, count(ps.att, NU * GROUPS, NU * g + u + 1))
                    act.activation(probs[:, u, :], prob_bank[u % 2][:], ACT.Exp,
                                   scale=scalar(exp_scale)).then_inc(prob_free, 1)

            def values(ps, g):
                act.wait_ge(o_ready, count(ps.att, GROUPS, g + 1))
                act.activation(ot_hi[:, g, :], o_sb[:], ACT.Copy).then_inc(o_hi_done, 1)

            def gate(ps, step):
                c, s = step[1], ps.slot(step)
                m = P if c < HC - 1 else HLAST
                act.wait_ge(work_full[s], ps.use(step))
                if c:
                    use = ("lin", c - 1)
                    act.wait_ge(work_free[ps.slot(use)], ps.use(use))
                act.activation(sig[0:m, :], work[s][0:m, :], ACT.Tanh,
                               scale=scalars[0:m, tanh_scale:tanh_scale + 1]).then_inc(tanh_done, 1)

            def lin(ps, c):
                m, use = P if c < HC - 1 else HLAST, ("lin", c)
                act.wait_ge(work_free[ps.slot(use)], ps.use(use))
                act.activation(g_hi[0:m, c, :], g32[c % 2][0:m, :], ACT.Copy).then_inc(g_hi_done, 1)

            def weight_sum(ps, m):
                n = WEIGHTS.index(m)
                act.wait_ge(raw_loaded, (32, 64, 80)[n])
                if n:
                    last = ("weight_turn", WEIGHTS[n - 1], HC - 1)
                    act.wait_ge(work_full[ps.slot(last)], ps.use(last))
                act.activation(nat[:, 0:raw_n[m]], raw[m], ACT.Abs, accum_out=scalar(abs_sum[m])).then_inc(abs_summed, 1)

            def weight_turn(ps, step):
                _, m, c = step
                s, cols = ps.slot(step), P if c < HC - 1 else HLAST
                src = work[s][:, 0:256].bitcast(F16).rearrange("p (k c) -> p k c", k=KC)
                act.wait_ge(work_full[s], ps.use(step))
                if m == "w2":
                    dst = t_down[0:cols, c, :].rearrange("p (k c) -> p k c", k=KC)
                    act.activation(dst, src[0:cols, :, :], ACT.Copy).then_inc(work_free[s], 1)
                else:
                    act.activation(t_up[m][:, :, c * P:c * P + cols], src[:, :, 0:cols], ACT.Copy).then_inc(work_free[s], 1)

            def run(ps):
                for step in ps.steps:
                    if step[0] == "xt":
                        turned_high(ps, step, xt_hi, step[1])
                    elif step[0] == "wo_split":
                        act.wait_ge(setup, 5)
                        act.activation(wo_hi[:], wo_raw, ACT.Copy, scale=scalar(wo_scale)).then_inc(weights_hi, 1)
                    elif step[0] == "yt":
                        turned_high(ps, step, yt_hi, step[1])
                    elif step[0] in ("q", "k"):
                        qk(ps, step)
                    elif step[0] == "v":
                        v(ps, step)
                    elif step[0] == "max_row":
                        max_row(ps, step)
                    elif step[0] == "probs":
                        exp(ps, step[1], step[2])
                    elif step[0] == "values":
                        values(ps, step[1])
                    elif step[0] == "gate":
                        gate(ps, step)
                    elif step[0] == "lin":
                        lin(ps, step[1])
                    elif step[0] == "weight_sum":
                        weight_sum(ps, step[1])
                    elif step[0] == "weight_turn":
                        weight_turn(ps, step)

            passes(act, run)

        @block.vector
        def _(dve):
            steps_done = [0]

            def scalar_step(ins):
                steps_done[0] += 1
                ins.then_inc(setup, 1)
                dve.wait_ge(setup, steps_done[0])

            def norm(n, b, src, dst, loaded):
                loaded()
                for i in range(ST):
                    dve.bn_stats(stats[n][:, i, :], src[:, i, :]).then_inc(stats_done[n], 1)
                dve.wait_ge(stats_done[n], count(b, ST, ST))
                dve.sem_inc(dve_passed, 1)
                for i in range(ST):
                    dve.bn_aggr(mean_var[n][:, i, :], stats[n][:, i, :]).then_inc(aggr_done[n], 1)
                dve.wait_ge(aggr_done[n], count(b, ST, ST))
                dve.tensor_scalar(var_eps[n][:], mean_var[n][:, :, 1], EPS, NORM_SCALE ** -2,
                                  ALU.add, ALU.mult).then_inc(var_done[n], 1)
                dve.wait_ge(rstd_done[n], count(b, 1, 1))
                for i in range(ST):
                    dve.tensor_scalar(dst[:, i, :], src[:, i, :], mean_var[n][:, i, 0:1], rstd[n][:, i:i + 1],
                                      ALU.subtract, ALU.mult).then_inc(norm_done[n], 1)

            for i in range(2):
                dve.memset(k_stack[i][3 * HD:P, :, :], MAX_UNIT).then_inc(consts_done, 1)
            norm("x", 0, xn, xn, lambda: dve.wait_ge(x_loaded, 16))
            for c in range(KC):
                dve.wait_ge(wqkv_loaded[c], 16)
                last = dve.tensor_reduce(scalar(wmax_part + c), wqkv_raw[:, c, :], AX_X, ALU.max,
                                         apply_absolute_value=True)
                last.then_inc(part_max_done, 1)
            dve.wait_ge(part_max_done, KC)
            dve.tensor_reduce(scalar(wmax_all), scalar(wmax_part, KC), AX_X, ALU.max).then_inc(wmax_done, 1)
            dve.wait_ge(reduced, 1)
            scalar_step(dve.tensor_scalar(scalar(tmp), scalar(wmax_all), 1e-30, 1.0 / WEIGHT_TOP, ALU.max, ALU.mult))
            scalar_step(dve.reciprocal(scalar(w_scale), scalar(tmp)))
            for c in range(KC):
                dve.wait_ge(weights_hi, c + 1)
                dve.scalar_tensor_tensor(wqkv_lo[:, c, :], wqkv_raw[:, c, :], scalar(w_scale), wqkv_hi[:, c, :],
                                         ALU.mult, ALU.subtract).then_inc(weights_split, 1)
            shrink = NORM_SCALE * QK_SHRINK
            scalar_step(dve.tensor_scalar(scalar(exp_scale), scalar(tmp), scalar(tmp), HD ** -0.5 / shrink ** 2,
                                          ALU.mult, ALU.mult))
            dve.wait_ge(consts_done, 7)
            dve.tensor_scalar(mask_rows[:], ident[:], -MASK, None, ALU.mult).then_inc(mask_scaled, 1)

            def wo_split():
                dve.wait_ge(wo_loaded, 16)
                dve.tensor_reduce(scalar(womax_all), wo_raw.rearrange("p c n -> p (c n)"), AX_X, ALU.max,
                                  apply_absolute_value=True).then_inc(wmax_done, 1)
                dve.wait_ge(reduced, 2)
                scalar_step(dve.tensor_scalar(scalar(womax_all), scalar(womax_all), 1e-30, 1.0 / WEIGHT_TOP, ALU.max, ALU.mult))
                scalar_step(dve.reciprocal(scalar(wo_scale), scalar(womax_all)))
                scalar_step(dve.tensor_scalar(scalar(project_scale), scalar(womax_all), scalar(tmp),
                                              1.0 / (NORM_SCALE * V_SHRINK), ALU.mult, ALU.mult))
                dve.wait_ge(weights_hi, KC + 1)
                dve.scalar_tensor_tensor(wo_lo[:], wo_raw, scalar(wo_scale), wo_hi[:],
                                         ALU.mult, ALU.subtract).then_inc(weights_split, 1)

            def turned_low(ps, step, hi, lo, i):
                s = ps.slot(step)
                cols = slice(i * P, (i + 1) * P)
                dve.wait_ge(work_half, ps.half(step))
                dve.tensor_tensor(lo[:, :, cols], work[s][:].rearrange("p (c s) -> p c s", c=KC), hi[:, :, cols],
                                  ALU.subtract).then_inc(work_free[s], 1)

            def qk(ps, step):
                g, s = step[1], ps.slot(step)
                pair = halves[g % 2]
                dve.wait_ge(work_half, ps.half(step))
                dve.scalar_tensor_tensor(pair[step[0] + "_lo"][:], work[s][:], QK_SHRINK, pair[step[0] + "_hi"][:],
                                         ALU.mult, ALU.subtract).then_inc(work_free[s], 1)

            def max_row(ps, step):
                s = ps.slot(step)
                dve.wait_ge(work_half, ps.half(step))
                dve.scalar_tensor_tensor(max_lo[:], work[s][0:HG * ST, 0:P], 1.0 / MAX_UNIT, max_hi[:],
                                         ALU.mult, ALU.subtract).then_inc(work_free[s], 1)

            def maxima(ps, g, p):
                for u in (2 * p, 2 * p + 1):
                    dve.wait_ge(score_full, count(ps.att, NU * GROUPS, NU * g + u + 1))
                    dve.tensor_reduce(block_max[:, u, :], score_bank[u % 2][:].rearrange("p (k c) -> p k c", c=P),
                                      AX_X, ALU.max).then_inc(score_free, 1)
                if p < PIECES - 1:
                    return
                dve.wait_ge(score_free, count(ps.att, NU * GROUPS, NU * (g + 1)))
                bm = block_max[:].rearrange("p (a r) k -> p a r k", a=2)
                nm = neg_max[:].rearrange("p (a h) t -> p a h t", a=2)
                dve.tensor_reduce(nm[:, :, :, 3], bm[:, :, 0:4:3, :], AX_X, ALU.max, negate=True).then_inc(max_ready, 1)
                dve.tensor_reduce(nm[:, :, :, 2], bm[:, :, 1:5:3, 0:3], AX_X, ALU.max, negate=True).then_inc(max_ready, 1)
                dve.tensor_reduce(nm[:, :, :, 1], bm[:, :, 2, :].rearrange("p a (h k) -> p a h k", h=2),
                                  AX_X, ALU.max, negate=True).then_inc(max_ready, 1)
                dve.tensor_scalar(nm[:, :, :, 0], bm[:, :, 1:5:3, 3], -1.0, None, ALU.mult).then_inc(max_ready, 1)

            def values(ps, g):
                dve.wait_ge(values_full, count(ps.att, GROUPS, g + 1))
                dve.reciprocal(inv_sum[:], sum_bank[:]).then_inc(inv_done, 1)
                dve.wait_ge(inv_done, count(ps.att, GROUPS, g + 1))
                if g or not ps.first:
                    dve.wait_ge(o_lo_done, count(ps.att, GROUPS, g))
                dve.tensor_tensor(o_sb[:], o_bank[:], inv_sum[:], ALU.mult).then_inc(o_ready, 1)

            def project(ps, step):
                i, s = step[1], ps.slot(step)
                dve.wait_ge(work_full[s], ps.use(step))
                dve.wait_ge(res_loaded[i], count(ps.att, 16, 16))
                dve.scalar_tensor_tensor(x_res[:, i, :], work[s][:], scalar(project_scale), x_res[:, i, :],
                                         ALU.mult, ALU.add).then_inc(work_free[s], 1)

            def gate(ps, step):
                c, s = step[1], ps.slot(step)
                m = P if c < HC - 1 else HLAST
                dve.wait_ge(tanh_done, count(ps.ffn, HC, c + 1))
                dve.scalar_tensor_tensor(sig[0:m, :], sig[0:m, :], 1.0, work[s][0:m, :],
                                         ALU.add, ALU.mult).then_inc(work_free[s], 1)

            def lin(ps, step):
                c, s = step[1], ps.slot(step)
                m = P if c < HC - 1 else HLAST
                dve.wait_ge(work_full[s], ps.use(step))
                before = ("gate", c)
                dve.wait_ge(work_free[ps.slot(before)], ps.use(before))
                if c >= 2:
                    dve.wait_ge(g_lo_done, count(ps.ffn, HC, c - 1))
                dve.scalar_tensor_tensor(g32[c % 2][0:m, :], sig[0:m, :], G_SHRINK, work[s][0:m, :],
                                         ALU.mult, ALU.mult).then_inc(work_free[s], 1)

            def down(ps, step):
                i, s = step[1], ps.slot(step)
                dve.wait_ge(work_full[s], ps.use(step))
                dve.scalar_tensor_tensor(x_res[:, i, :], work[s][:], scalar(down_scale), x_res[:, i, :],
                                         ALU.mult, ALU.add).then_inc(work_free[s], 1)

            def weight_load(m):
                if m == "w1":
                    dve.wait_ge(weights_split, KC + 1)
                    dve.memset(raw_rows[:, HC - 1, :], 0.0).then_inc(pad_zeroed, 1)

            def weight_ternary(m):
                n, size = WEIGHTS.index(m), raw_n[m]
                dve.wait_ge(reduced, 3 + n)
                scalar_step(dve.tensor_scalar(scalar(half_s[m]), scalar(abs_all[m]), 0.5 / (HIDDEN * D), None, ALU.mult))
                scalar_step(dve.tensor_scalar(scalar(neg_half_s[m]), scalar(half_s[m]), -1.0, None, ALU.mult))
                if m == "w1":
                    scalar_step(dve.tensor_scalar(scalar(tanh_scale), scalar(half_s[m]), 1.0 / NORM_SCALE, None, ALU.mult))
                if m == "w2":
                    k = 8.0 / (2.0 * NORM_SCALE ** 2 * G_SHRINK)
                    scalar_step(dve.tensor_scalar(scalar(down_scale), scalar(half_s["w1"]), scalar(half_s["w3"]), k,
                                                  ALU.mult, ALU.mult))
                    scalar_step(dve.tensor_scalar(scalar(down_scale), scalar(down_scale), scalar(half_s[m]), None, ALU.mult))
                for part in range(TERNARY_PARTS):
                    a, z = part * BELOW, min(size, (part + 1) * BELOW)
                    done = TERNARY_PARTS * n + part
                    if done:
                        dve.wait_ge(ternary_done, done)
                    dve.tensor_scalar(below[:, 0:z - a], raw[m][:, a:z], scalar(neg_half_s[m]), None,
                                      ALU.is_lt).then_inc(below_done, 1)
                    dve.wait_ge(below_done, done + 1)
                    dve.scalar_tensor_tensor(nat[:, a:z], raw[m][:, a:z], scalar(half_s[m]), below[:, 0:z - a],
                                             ALU.is_gt, ALU.subtract).then_inc(ternary_done, 1)

            def run(ps):
                for step in ps.steps:
                    if step[0] == "xt":
                        turned_low(ps, step, xt_hi, xt_lo, step[1])
                    elif step[0] == "wo_split":
                        wo_split()
                    elif step[0] == "yt":
                        turned_low(ps, step, yt_hi, yt_lo, step[1])
                    elif step[0] in ("q", "k"):
                        qk(ps, step)
                    elif step[0] == "max_row":
                        max_row(ps, step)
                    elif step[0] == "scores":
                        maxima(ps, step[1], step[2])
                    elif step[0] == "values":
                        values(ps, step[1])
                    elif step[0] == "project":
                        project(ps, step)
                    elif step[0] == "norm_x":
                        b = ps.att + 1
                        norm("x", b, xn, xn, lambda: dve.wait_ge(x_loaded, count(b, 16, 16)))
                    elif step[0] == "norm_y":
                        def projected():
                            for i in (ST - 2, ST - 1):
                                use = ("project", i)
                                dve.wait_ge(work_free[ps.slot(use)], ps.use(use))
                        norm("y", ps.att, x_res, yn, projected)
                    elif step[0] == "gate":
                        gate(ps, step)
                    elif step[0] == "lin":
                        lin(ps, step)
                    elif step[0] == "down":
                        down(ps, step)
                    elif step[0] == "weight_load":
                        weight_load(step[1])
                    elif step[0] == "weight_ternary":
                        weight_ternary(step[1])

            passes(dve, run)

        @block.tensor
        def _(pe):
            pe.wait_ge(consts_done, 7)

            def open_work(ps, step):
                s, k = ps.slot(step), ps.use(step) - 1
                if not (isinstance(k, int) and k == 0):
                    pe.wait_ge(work_free[s], k)
                return s

            def evacuated(ps, step):
                pe.wait_ge(work_free[ps.slot(step)], ps.use(step))

            def products(bank, terms):
                for n, (lhs, rhs) in enumerate(terms):
                    last = pe.matmul(bank, lhs, rhs, start=(n == 0), stop=(n == len(terms) - 1))
                return last

            def turn(ps, step, src, ready, b):
                i = step[1]
                s = open_work(ps, step)
                pe.wait_ge(ready, count(b, ST, i + 1))
                for c in range(KC):
                    last = pe.transpose(work[s][:, c * P:(c + 1) * P], src[:, i, c * P:(c + 1) * P], ident[:])
                last.then_inc(work_full[s], 1)

            def split_terms(a_hi, a_lo, b_hi, b_lo):
                return [(a_hi, b_hi), (a_hi, b_lo), (a_lo, b_hi)]

            def qk(ps, step):
                g = step[1]
                s = open_work(ps, step)
                if step == ("q", 0):
                    evacuated(ps, ("xt", ST - 1))
                    evacuated(ps, ("xt", ST - 2))
                cols = slice((step[0] == "k") * D + g * P, (step[0] == "k") * D + (g + 1) * P)
                for c in range(KC):
                    if ps.first and step == ("q", 0):
                        pe.wait_ge(weights_split, c + 1)
                    for n, (w, xx) in enumerate(split_terms(wqkv_hi, wqkv_lo, xt_hi, xt_lo)):
                        last = pe.matmul(work[s][:], w[:, c, cols], xx[:, c, :],
                                         start=(c == 0 and n == 0), stop=(c == KC - 1 and n == 2))
                last.then_inc(work_full[s], 1)

            def v(ps, step):
                i = step[1]
                s = open_work(ps, step)
                rows = slice(i * P, (i + 1) * P)
                terms = []
                for c in range(KC):
                    terms += [(a[:, c, rows], w[:, c, 2 * D:3 * D])
                              for a, w in split_terms(xt_hi, xt_lo, wqkv_hi, wqkv_lo)]
                products(work[s][:], terms).then_inc(work_full[s], 1)

            def scores(ps, g, p):
                if p == 0:
                    pe.wait_ge(stacked[g % 2], count(ps.att, 32 * STACK_DMAS, 16 * STACK_DMAS * (g // 2 + 1)))
                    if g == 0 and ps.first:
                        pe.wait_ge(mask_scaled, 1)
                q, k = q_stack[g % 2], k_stack[g % 2]
                for u in (2 * p, 2 * p + 1):
                    if u >= 2 or g or not ps.first:
                        pe.wait_ge(score_free, count(ps.att, NU * GROUPS, NU * g + u - 1))
                    bank = score_bank[u % 2]
                    for h, tile, off, n in UNITS[u]:
                        pe.matmul(bank[:, off:off + n], q[0:3 * HD, h, tile * P:(tile + 1) * P],
                                  k[0:3 * HD, h, 0:n], start=True, stop=False)
                        last = pe.matmul(bank[:, off + n - P:off + n], mask_rows[:], mask_cols[:],
                                         start=False, stop=True)
                    last.then_inc(score_full, 1)

            def max_row(ps, step):
                g = step[1]
                s = open_work(ps, step)
                pe.wait_ge(max_ready, count(ps.att, 4 * GROUPS, 4 * g + 4))
                pe.transpose(work[s][0:HG * ST, 0:P], neg_max[:].rearrange("p h t -> p (h t)"),
                             ident[:]).then_inc(work_full[s], 1)

            def probs_(ps, g, p):
                if p == 0:
                    pe.wait_ge(max_placed[g % 2], count(ps.att, 64, 32 * (g // 2 + 1)))
                q, k = q_stack[g % 2], k_stack[g % 2]
                rows = 3 * HD + 2
                for u in (2 * p, 2 * p + 1):
                    if u >= 2 or g or not ps.first:
                        pe.wait_ge(prob_free, count(ps.att, NU * GROUPS, NU * g + u - 1))
                    bank = prob_bank[u % 2]
                    for h, tile, off, n in UNITS[u]:
                        kt = ST - 1 - tile
                        last = pe.matmul(bank[:, off:off + n], k[0:rows, h, kt * P:(kt + 1) * P],
                                         q[0:rows, h, S - n:S], start=True, stop=True)
                    last.then_inc(prob_full, 1)

            def values(ps, g):
                if g == 0:
                    evacuated(ps, ("v", ST - 2))
                    evacuated(ps, ("v", ST - 1))
                pe.wait_ge(selected, count(ps.att, SELECTS * GROUPS, SELECTS * (g + 1)))
                if g or not ps.first:
                    pe.wait_ge(o_ready, count(ps.att, GROUPS, g))
                for kt in range(ST):
                    for bank, ones_side in ((o_bank, False), (sum_bank, True)):
                        for h in range(HG):
                            u, off, n = [(u, off, n) for u in range(NU) for hh, tile, off, n in UNITS[u]
                                         if (hh, tile) == (h, ST - 1 - kt)][0]
                            col = (g * HG + h) * HD
                            lhs = ones[:] if ones_side else v_sb[:, kt, col:col + HD]
                            last = pe.matmul(bank[HD * h:HD * (h + 1), S - n:S], lhs, probs[:, u, off:off + n],
                                             start=(kt == 0), stop=(kt == ST - 1), skip_group_check=True)
                last.then_inc(values_full, 1)

            def project(ps, step):
                i = step[1]
                s = open_work(ps, step)
                if i == 0:
                    pe.wait_ge(o_lo_done, count(ps.att, GROUPS, GROUPS))
                    if ps.first:
                        pe.wait_ge(weights_split, KC + 1)
                rows = slice(i * P, (i + 1) * P)
                terms = []
                for c in range(GROUPS):
                    terms += [(a[:, c, rows], w[:, c, :]) for a, w in split_terms(ot_hi, ot_lo, wo_hi, wo_lo)]
                products(work[s][:], terms).then_inc(work_full[s], 1)

            def up(ps, step):
                c = step[1]
                m = P if c < HC - 1 else HLAST
                s = open_work(ps, step)
                if step == ("gate", 0):
                    evacuated(ps, ("yt", ST - 1))
                    evacuated(ps, ("yt", ST - 2))
                w = t_up["w1" if step[0] == "gate" else "w3"]
                terms = [(w[:, k, c * P:c * P + m], y[:, k, :]) for k in range(KC) for y in (yt_hi, yt_lo)]
                products(work[s][0:m, :], terms).then_inc(work_full[s], 1)

            def down(ps, step):
                i = step[1]
                s = open_work(ps, step)
                if i == 0:
                    pe.wait_ge(g_lo_done, count(ps.ffn, HC, HC))
                terms = []
                for c in range(HC):
                    m = P if c < HC - 1 else HLAST
                    terms += [(g[0:m, c, i * P:(i + 1) * P], t_down[0:m, c, :]) for g in (g_hi, g_lo)]
                products(work[s][:], terms).then_inc(work_full[s], 1)

            def weight_turn(ps, step):
                _, m, c = step
                s = open_work(ps, step)
                cols = P if c < HC - 1 else HLAST
                bank = work[s][:, 0:256].bitcast(F16)
                if c == 0:
                    pe.wait_ge(ternary_done, TERNARY_PARTS * (WEIGHTS.index(m) + 1))
                for k in range(KC):
                    if m == "w2":
                        src = nat[:, 0:ST * HIDDEN].rearrange("p (k n) -> p k n", k=ST)[:, k, c * P:c * P + cols]
                        last = pe.transpose(bank[0:cols, k * P:(k + 1) * P], src, ident16[:])
                    else:
                        src = nat[:, c * D + k * P:c * D + (k + 1) * P]
                        last = pe.transpose(bank[:, k * P:(k + 1) * P], src, ident16[:])
                last.then_inc(work_full[s], 1)

            def run(ps):
                for step in ps.steps:
                    if step[0] == "xt":
                        turn(ps, step, xn, norm_done["x"], ps.att)
                    elif step[0] == "yt":
                        turn(ps, step, yn, norm_done["y"], ps.ffn)
                    elif step[0] in ("q", "k"):
                        qk(ps, step)
                    elif step[0] == "v":
                        v(ps, step)
                    elif step[0] == "scores":
                        scores(ps, step[1], step[2])
                    elif step[0] == "max_row":
                        max_row(ps, step)
                    elif step[0] == "probs":
                        probs_(ps, step[1], step[2])
                    elif step[0] == "values":
                        values(ps, step[1])
                    elif step[0] == "project":
                        project(ps, step)
                    elif step[0] in ("gate", "lin"):
                        up(ps, step)
                    elif step[0] == "down":
                        down(ps, step)
                    elif step[0] == "weight_turn":
                        weight_turn(ps, step)

            passes(pe, run)


_INS = ["L0_attn_x", "L0_attn_Wqkv", "L0_attn_Wo", "L0_ffn_w1", "L0_ffn_w3", "L0_ffn_w2"]


def kernel(**inputs):
    import numpy as np
    import concourse.bacc as bacc
    from concourse.bass_utils import run_bass_kernel_spmd

    nc = bacc.Bacc("TRN2", target_bir_lowering=False, num_devices=1)
    arrays, args = {}, []
    for name in _INS:
        a = np.ascontiguousarray(inputs[name])
        arrays[f"in_{name}"] = a
        args.append(nc.dram_tensor(f"in_{name}", a.shape, mybir.dt.from_np(a.dtype), kind="ExternalInput").ap())
    out = nc.dram_tensor("out_y", (BATCHES, S, D), F32, kind="ExternalOutput").ap()
    build(nc, *args, out)
    r = run_bass_kernel_spmd(nc, [arrays], core_ids=[0])
    return r.results[0]["out_y"]
```

```python
from contextlib import ExitStack

import concourse.bass as bass
from concourse import mybir

F32 = mybir.dt.float32
F16 = mybir.dt.float16
ACT = mybir.ActivationFunctionType
ALU = mybir.AluOpType
AX_X = mybir.AxisListType.X
RMAX = bass.bass_isa.ReduceOp.max
RADD = bass.bass_isa.ReduceOp.add

P = 128
D = 512
S = 512
BATCHES = 4
HD = 32
HEADS = D // HD
HG = P // HD
GROUPS = HEADS // HG
KC = D // P
ST = S // P
HIDDEN = int(2 * D * 4 / 3)
HC = -(-HIDDEN // P)
HLAST = HIDDEN - (HC - 1) * P
EPS = 1e-5

NORM_SCALE = 16.0
WEIGHT_TOP = 64.0
QK_SHRINK = 1.0 / 128
V_SHRINK = 1.0 / 16
MAX_UNIT = 32768.0
MASK = 60000.0
ROUND = 1.5 * 2.0 ** 23
G_SHRINK = 1.0 / 4096

UNITS = []
for pair in range(HG // 2):
    h = 2 * pair
    UNITS += [[(h, 3, 0, 512)], [(h, 2, 0, 384), (h, 0, 384, 128)],
              [(h, 1, 0, 256), (h + 1, 1, 256, 256)],
              [(h + 1, 3, 0, 512)], [(h + 1, 2, 0, 384), (h + 1, 0, 384, 128)]]
NU = len(UNITS)
PIECES = NU // 2
SELECTS = 6

WEIGHTS = ("w1", "w3", "w2")
LAG = 3
PARTS = 4


def part(m, j):
    if m == "w2":
        return j, j + 1, HIDDEN
    return 3 * j, min(HC, 3 * j + 3), D


def chunks_under(m, j):
    _, end, cols = part(m, j)
    return -(-end * cols // D)


def order(attend, feed, prefetch, prepare):
    o = []
    fillers = []
    if feed:
        for c in range(HC):
            fillers += [[("gate", c)], [("lin", c)]]
    if prepare:
        for m, after in zip(WEIGHTS, WEIGHTS[1:] + (None,)):
            for c in range(HC):
                fillers.append([("weight_round", m, c)])
                if c:
                    fillers[-1].append(("weight_ternary", m, c - 1))
                if c >= LAG:
                    fillers[-1].append(("weight_turn", m, c - LAG))
                if after:
                    fillers[-1] += [("weight_load", after, j) for j in range(PARTS) if chunks_under(after, j) == c]
                    fillers[-1] += [("weight_sum", after, j) for j in range(2) if chunks_under(after, j) == c - 3]
            fillers += [[("weight_turn", m, c)] for c in range(HC - LAG, HC)]
            fillers[-LAG].insert(0, ("weight_ternary", m, HC - 1))
            if after:
                fillers[-LAG].append(("weight_load", after, PARTS - 1))
                fillers[-2].append(("weight_sum", after, 2))
                fillers += [[("weight_sum", after, 3)], [], []]
    rate = 2 if prepare else 1

    def fill(k):
        for _ in range(k * rate):
            if fillers:
                o.extend(fillers.pop(0))

    if not attend:
        o += [("norm_y", i) for i in range(ST)] + [("yt", i) for i in range(ST)]
        fill(len(fillers))
        return o + [("down", i) for i in range(ST)]
    if prepare:
        o += [("xt", i) for i in range(ST)]
        o.append(("weight_split",))
    o += [("q", 0), ("place", "q", 0)]
    if prepare:
        o.append(("wo_max",))
    o += [("k", 0), ("place", "k", 0)]
    if prefetch:
        o.append(("x_load",))
    if prepare:
        o += [("weight_load", WEIGHTS[0], j) for j in range(PARTS)]
    if feed:
        o += [("norm_y", i) for i in range(ST)]
    o.append(("v", 0))
    if prepare:
        o.append(("wo_split",))
    o += [("v", i) for i in range(1, ST)]
    if prepare:
        o += [("weight_sum", WEIGHTS[0], j) for j in range(2)]
    for p in range(PIECES):
        o.append(("scores", 0, p))
        if p in (2, 4):
            o.append(("place", "q" if p == 2 else "k", 1))
        if p in (1, 3):
            o.append(("q" if p == 1 else "k", 1))
        elif feed and p < PIECES - 1:
            o += [("yt", p), ("yt", p + 1)]
        if prepare and p in (0, 2):
            o.append(("unit_rows", p // 2))
        if prepare and p == 1:
            o += [("weight_sum", WEIGHTS[0], j) for j in range(2, PARTS)]
    fill(1)
    o.append(("max_row", 0))
    fill(2)
    for g in range(GROUPS - 1):
        for p in range(PIECES):
            o += [("scores", g + 1, p), ("probs", g, p)]
            if p in (1, 3) and g + 2 < GROUPS:
                o.append(("place", "q" if p == 1 else "k", g + 2))
            if prepare and g == 0 and p == 1:
                o.append(("unit_rows", 2))
            if p in (0, 2) and g + 2 < GROUPS:
                o.append(("q" if p == 0 else "k", g + 2))
            else:
                fill(1)
            if g == GROUPS - 2 and prefetch and p < ST:
                o.append(("stats_x", p))
        fill(1)
        o += [("max_row", g + 1), ("values", g)]
    for p in range(PIECES):
        o.append(("probs", GROUPS - 1, p))
        if prefetch and p < ST:
            o.append(("norm_x", p))
        fill(2 if p == 0 else 1)
    fill(len(fillers))
    if feed:
        o += [("down", 0), ("down", 1)]
    o.append(("values", GROUPS - 1))
    if feed:
        o += [("down", 2), ("down", 3)]
    if prefetch:
        o += [("xt_next", 0), ("xt_next", 1)]
    for i in range(ST):
        o.append(("project", i))
        if prefetch and i < 2:
            o.append(("xt_next", 2 + i))
        o.append(("stats_y", i))
    return o


HALF_STEPS = ("xt", "xt_next", "yt", "q", "k", "max_row")
WORK_STEPS = ("xt", "xt_next", "yt", "q", "k", "v", "max_row", "project", "gate", "lin", "down", "weight_turn")


def numbered(steps, kinds):
    found = [s for s in steps if s[0] in kinds]
    return {s: n for n, s in enumerate(found)}


def from_end(steps, step):
    uses = numbered(steps, WORK_STEPS)
    return len(uses) - uses[step]


FIRST = order(True, False, True, True)
MIDDLE = order(True, True, True, False)
LAST_ATTENTION = order(True, True, False, False)
LAST = order(False, True, False, False)


class Pass:

    def __init__(self, steps, att, ffn, before=(), rounds=0):
        self.steps, self.att, self.ffn, self.rounds = steps, att, ffn, rounds
        self.first = steps is FIRST
        self.steps_before = before[-1] if before else None
        self.uses, self.halves = numbered(steps, WORK_STEPS), numbered(steps, HALF_STEPS)
        self.uses_before = sum(len(numbered(s, WORK_STEPS)) for s in before)
        self.halves_before = sum(len(numbered(s, HALF_STEPS)) for s in before)

    def slot(self, step):
        return (self.uses_before + self.uses[step]) % 2

    def use(self, step):
        k = (self.uses_before + self.uses[step]) // 2 + 1
        return k if isinstance(self.rounds, int) and self.rounds == 0 else self.rounds * (MIDDLE_USES // 2) + k

    def previous(self, step):
        n = self.uses_before - from_end(self.steps_before, step)
        k = n // 2 + 1
        return n % 2, k if isinstance(self.rounds, int) and self.rounds == 0 else self.rounds * (MIDDLE_USES // 2) + k

    def half(self, step):
        k = self.halves_before + self.halves[step] + 1
        return k if isinstance(self.rounds, int) and self.rounds == 0 else self.rounds * MIDDLE_HALVES + k


MIDDLE_USES = len(numbered(MIDDLE, WORK_STEPS))
MIDDLE_HALVES = len(numbered(MIDDLE, HALF_STEPS))
assert MIDDLE_USES % 2 == 0
for s in [("project", i) for i in range(ST)] + [("xt_next", i) for i in range(ST)]:
    assert from_end(FIRST, s) == from_end(MIDDLE, s)


def passes(engine, run):
    run(Pass(FIRST, 0, None))
    with engine.Fori(1, BATCHES - 1) as t:
        run(Pass(MIDDLE, t, t - 1, [FIRST], t - 1))
    before = [FIRST] + [MIDDLE] * (BATCHES - 2)
    run(Pass(LAST_ATTENTION, BATCHES - 1, BATCHES - 2, before))
    run(Pass(LAST, None, BATCHES - 1, before + [LAST_ATTENTION]))


def build(nc, x, wqkv, wo, w1, w3, w2, out):
    x_v = x.rearrange("b (i p) d -> b p i d", p=P)
    out_v = out.rearrange("b (i p) d -> b p i d", p=P)
    wqkv_v = wqkv.rearrange("(c p) n -> p c n", p=P)
    wo_v = wo.rearrange("(c p) n -> p c n", p=P)
    w_dram = {"w1": w1, "w3": w3, "w2": w2}

    with ExitStack() as ctx:
        def sb(name, shape, dt):
            return ctx.enter_context(nc.sbuf_tensor(name, shape, dt))

        def psum(name, shape, dt):
            return ctx.enter_context(nc.psum_tensor(name, shape, dt))

        def sem(name):
            return ctx.enter_context(nc.semaphore(name))

        wqkv_hi = sb("wqkv_hi", [P, KC, 3 * D], F16)
        wqkv_lo = sb("wqkv_lo", [P, KC, 3 * D], F16)
        wo_hi = sb("wo_hi", [P, KC, D], F16)
        wo_lo = sb("wo_lo", [P, KC, D], F16)
        t_up = {m: sb(f"{m}_ternary", [P, KC, HIDDEN], F16) for m in ("w1", "w3")}
        t_down = sb("w2_ternary", [P, HC, D], F16)
        ident = sb("ident", [P, P], F32)
        ident16 = sb("ident16", [P, P], F16)
        mask_rows = sb("mask_rows", [P, P], F16)
        mask_cols = sb("mask_cols", [P, P], F16)
        ones = sb("ones", [P, HD], F32)
        neg_half = sb("neg_half", [P, ST], F32)
        scalars = sb("scalars", [P, 64], F32)
        xn = sb("xn", [P, ST, D], F32)
        x_res = sb("x_res", [P, ST, D], F32)
        xt_hi = sb("xt_hi", [P, KC, S], F16)
        xt_lo = sb("xt_lo", [P, KC, S], F16)
        v_sb = sb("v_sb", [P, ST, D], F32)
        half_hi = sb("half_hi", [P, S], F16)
        half_lo = sb("half_lo", [P, S], F16)
        stack_of = [0, 1, 2, 0]
        q_stack = [sb(f"q_stack{i}", [P, HG, S], F16) for i in range(3)]
        k_stack = [sb(f"k_stack{i}", [P, HG, S], F16) for i in range(3)]
        block_max = sb("block_max", [P, NU, 4], F32)
        neg_max = sb("neg_max", [P, HG, ST], F32)
        max_hi = sb("max_hi", [HG * ST, P], F16)
        max_lo = sb("max_lo", [HG * ST, P], F16)
        probs = sb("probs", [P, NU, 512], F32)
        inv_sum = sb("inv_sum", [P, S], F32)
        o_sb = sb("o_sb", [P, S], F32)
        ot_hi = sb("ot_hi", [P, GROUPS, S], F16)
        ot_lo = sb("ot_lo", [P, GROUPS, S], F16)
        stats = {n: sb(f"{n}_stats", [P, ST, 6], F32) for n in "xy"}
        mean_var = {n: sb(f"{n}_mean_var", [P, ST, 2], F32) for n in "xy"}
        var_eps = {n: sb(f"{n}_var_eps", [P, ST], F32) for n in "xy"}
        rstd = {n: sb(f"{n}_rstd", [P, ST], F32) for n in "xy"}
        RAW = HC * D
        late = sb("late", [P, 36864 // 4], F32)
        g_hi = late[:, 0:HC * S // 2].bitcast(F16).rearrange("p (c s) -> p c s", c=HC)
        g_lo = late[:, HC * S // 2:HC * S].bitcast(F16).rearrange("p (c s) -> p c s", c=HC)
        yt_hi = late[:, RAW:RAW + 1024].bitcast(F16).rearrange("p (c s) -> p c s", c=KC)
        yt_lo = late[:, RAW + 1024:RAW + 2048].bitcast(F16).rearrange("p (c s) -> p c s", c=KC)
        sig = late[:, RAW + 2048:RAW + 2560]
        g32 = [late[:, RAW + 2560:RAW + 3072], late[:, RAW + 3072:RAW + 3584]]
        yn = sb("yn", [P, ST, D], F32)
        wqkv_raw = late[:, 0:KC * 3 * D].rearrange("p (c n) -> p c n", c=KC)
        wo_raw = late[:, KC * 3 * D:KC * 4 * D].rearrange("p (c n) -> p c n", c=KC)
        raw_rows = late[:, 0:HC * D].rearrange("p (c n) -> p c n", c=HC)
        raw_down = late[:, 0:ST * HIDDEN].rearrange("p (c n) -> p c n", c=ST)
        raw = {"w1": late[:, 0:HC * D], "w3": late[:, 0:HC * D], "w2": late[:, 0:ST * HIDDEN]}
        nat = late[:, HC * D:HC * D + HC * D // 2].bitcast(F16)
        magnitudes = yn[:].rearrange("p i d -> p (i d)").bitcast(F16)[:, 0:3 * D]

        def chunk_views(m, c):
            cols = P if c < HC - 1 else HLAST
            if m == "w2":
                return [t.rearrange("p (k n) -> p k n", k=ST)[:, :, c * P:c * P + cols]
                        for t in (raw[m], nat[:, 0:ST * HIDDEN])]
            return raw[m][:, c * D:(c + 1) * D], nat[:, c * D:(c + 1) * D]

        def raw_part(m, j):
            a, z, cols = part(m, j)
            return raw[m][:, a * cols:z * cols]

        def scalar(i, n=1):
            return scalars[:, i:i + n]
        wmax_part, wmax_all, w_scale, womax_all, wo_scale = 0, 4, 5, 7, 8
        exp_scale, project_scale, down_scale, tanh_scale, tmp = 9, 10, 11, 12, 13
        abs_part = {"w1": 32, "w3": 36, "w2": 40}
        abs_part_all = {"w1": 44, "w3": 48, "w2": 52}
        abs_all = {"w1": 17, "w3": 18, "w2": 19}
        half_s = {"w1": 20, "w3": 21, "w2": 22}
        inv_s = {"w1": 23, "w3": 24, "w2": 25}
        neg_round = 26

        work = [psum(f"work{i}", [P, 512], F32) for i in range(2)]
        score_bank = [psum(f"score_bank{i}", [P, 512], F32) for i in range(2)]
        prob_bank = [psum(f"prob_bank{i}", [P, 512], F32) for i in range(2)]
        o_bank = psum("o_bank", [P, S], F32)
        sum_bank = psum("sum_bank", [P, S], F32)

        x_first_loaded = [sem(f"x_first_loaded{i}") for i in range(ST)]
        x_loaded = sem("x_loaded")
        res_loaded = [sem(f"res_loaded{i}") for i in range(ST)]
        wqkv_loaded = [sem(f"wqkv_loaded{i}") for i in range(KC)]
        wo_loaded = sem("wo_loaded")
        raw_loaded = [sem(f"raw_loaded{j}") for j in range(PARTS)]
        out_stored = [sem(f"out_stored{i}") for i in range(ST)]
        hi_placed = sem("hi_placed")
        lo_placed = sem("lo_placed")
        stacked = [sem(f"stacked{g}") for g in range(GROUPS)]
        max_placed = [sem(f"max_placed{g}") for g in range(GROUPS)]
        stats_done = {n: sem(f"{n}_stats_done") for n in "xy"}
        aggr_done = {n: sem(f"{n}_aggr_done") for n in "xy"}
        var_done = {n: sem(f"{n}_var_done") for n in "xy"}
        rstd_done = {n: sem(f"{n}_rstd_done") for n in "xy"}
        norm_done = {n: sem(f"{n}_norm_done") for n in "xy"}
        work_full = [sem(f"work_full{i}") for i in range(2)]
        work_free = [sem(f"work_free{i}") for i in range(2)]
        work_half = sem("work_half")
        score_full = sem("score_full")
        score_free = sem("score_free")
        max_ready = sem("max_ready")
        prob_full = sem("prob_full")
        prob_free = sem("prob_free")
        selected = sem("selected")
        sums_full = sem("sums_full")
        values_full = sem("values_full")
        inv_done = sem("inv_done")
        o_ready = sem("o_ready")
        o_hi_done = sem("o_hi_done")
        o_lo_done = sem("o_lo_done")
        tanh_done = sem("tanh_done")
        g_hi_done = sem("g_hi_done")
        g_lo_done = sem("g_lo_done")
        sp_passed, pool_passed, dve_passed = (sem(n) for n in ("sp_passed", "pool_passed", "dve_passed"))
        zeroed = sem("zeroed")
        consts_done = sem("consts_done")
        unit_rows_set = sem("unit_rows_set")
        mask_scaled = sem("mask_scaled")
        part_max_done = sem("part_max_done")
        wmax_done = sem("wmax_done")
        reduced = sem("reduced")
        setup = sem("setup")
        weights_hi = sem("weights_hi")
        weights_split = sem("weights_split")
        pad_zeroed = sem("pad_zeroed")
        abs_summed = sem("abs_summed")
        rounded = sem("rounded")
        ternary_done = sem("ternary_done")

        def count(b, per, k):
            return b * per + k

        block = ctx.enter_context(nc.Block())

        @block.sync
        def _(sp):
            def wait(semaphore, value):
                sp.wait_ge(semaphore, value)
                sp.sem_inc(sp_passed, 1)

            for i in range(ST):
                sp.dma_start(xn[:, i, :], x_v[0, :, i, :]).then_inc(x_first_loaded[i], 16)
            for c in range(KC):
                sp.dma_start(wqkv_raw[:, c, :], wqkv_v[:, c, :]).then_inc(wqkv_loaded[c], 16)
            sp.dma_start(wo_raw, wo_v).then_inc(wo_loaded, 16)
            for i in range(ST):
                sp.dma_start(x_res[:, i, :], x_v[0, :, i, :]).then_inc(res_loaded[i], 16)

            def x_load(ps):
                wait(work_full[ps.slot(("q", 0))], ps.use(("q", 0)))
                sp.dma_start(xn[:], x_v[ps.att + 1]).then_inc(x_loaded, 16)

            def stack(ps, g):
                i = stack_of[g]
                wait(hi_placed, count(ps.att, 2 * GROUPS, 2 * g + 2))
                wait(lo_placed, count(ps.att, 2 * GROUPS, 2 * g + 2))
                sp.dma_start(q_stack[i][2 * HD:3 * HD, :, :], q_stack[i][0:HD, :, :]).then_inc(stacked[g], 16)
                sp.dma_start(k_stack[i][HD:2 * HD, :, :], k_stack[i][0:HD, :, :]).then_inc(stacked[g], 16)

            def max_row(ps, g):
                use = ("max_row", g)
                wait(work_free[ps.slot(use)], ps.use(use))
                for j, src in enumerate((max_hi, max_lo)):
                    dst = q_stack[stack_of[g]][3 * HD + j:3 * HD + j + 1, :, :].rearrange("o h (t q) -> o (h t) q", q=P)
                    sp.dma_start(dst, src[:]).then_inc(max_placed[g], 16)

            def down(ps, i):
                use = ("down", i)
                wait(work_free[ps.slot(use)], ps.use(use))
                sp.dma_start(out_v[ps.ffn, :, i, :], x_res[:, i, :]).then_inc(out_stored[i], 16)
                if ps.att is not None:
                    wait(out_stored[i], count(ps.ffn, 16, 16))
                    sp.dma_start(x_res[:, i, :], x_v[ps.att, :, i, :]).then_inc(res_loaded[i], 16)

            def weight_load(m, j):
                n = WEIGHTS.index(m)
                a, z, _ = part(m, j)
                if n == 0:
                    sp.wait_ge(weights_split, KC)
                    if j == PARTS - 1:
                        sp.wait_ge(pad_zeroed, 1)
                else:
                    sp.wait_ge(ternary_done, HC * (n - 1) + chunks_under(m, j))
                if m == "w2":
                    sp.dma_start(raw_down[:, a:z, :],
                                 w2.rearrange("(c p) n -> p c n", p=P)[:, a:z, :]).then_inc(raw_loaded[j], 16)
                    return
                full = min(z, HC - 1)
                sp.dma_start(raw_rows[:, a:full, :],
                             w_dram[m][a * P:full * P, :].rearrange("(c p) n -> p c n", p=P)).then_inc(raw_loaded[j], 16)
                if z == HC:
                    sp.dma_start(raw_rows[0:HLAST, HC - 1, :], w_dram[m][(HC - 1) * P:HIDDEN, :]).then_inc(raw_loaded[j], 16)

            def run(ps):
                for step in ps.steps:
                    if step[0] == "x_load":
                        x_load(ps)
                    elif step[0] == "place" and step[1] == "k":
                        stack(ps, step[2])
                    elif step[0] == "max_row":
                        max_row(ps, step[1])
                    elif step[0] == "down":
                        down(ps, step[1])
                    elif step[0] == "weight_load":
                        weight_load(step[1], step[2])

            passes(sp, run)
            for i in range(ST):
                sp.wait_ge(out_stored[i], 16 * BATCHES)

        @block.gpsimd
        def _(pool):
            pool.memset(ident[:], 0.0).then_inc(zeroed, 1)
            pool.memset(ident16[:], 0.0).then_inc(zeroed, 1)
            pool.memset(mask_cols[:], 0.0).then_inc(zeroed, 1)
            pool.memset(ones[:], 1.0).then_inc(consts_done, 1)
            pool.memset(neg_half[:], -0.5).then_inc(consts_done, 1)
            pool.wait_ge(zeroed, 3)
            for t in (ident, ident16):
                pool.affine_select(out=t[:], in_=t[:], compare_op=ALU.not_equal, fill=1.0, base=0,
                                   pattern=[[-1, P]], channel_multiplier=1).then_inc(consts_done, 1)
            pool.affine_select(out=mask_cols[:], in_=mask_cols[:], compare_op=ALU.is_ge, fill=MASK, base=0,
                               pattern=[[-1, P]], channel_multiplier=1).then_inc(consts_done, 1)

            def power(n, b, i):
                pool.wait_ge(var_done[n], count(b, ST, i + 1))
                pool.tensor_tensor(rstd[n][:, i:i + 1], var_eps[n][:, i:i + 1], neg_half[:, 0:1],
                                   ALU.pow).then_inc(rstd_done[n], 1)

            def all_reduce(dst, src, op, n=1):
                pool.partition_all_reduce(scalar(dst, n), scalar(src, n), P, op).then_inc(reduced, 1)

            pool.wait_ge(consts_done, 6)
            for i in range(ST):
                power("x", 0, i)
            pool.wait_ge(wmax_done, 1)
            all_reduce(wmax_all, wmax_all, RMAX)
            pool.wait_ge(wmax_done, 2)
            all_reduce(womax_all, womax_all, RMAX)

            def select(ps, g, p):
                pairs = {2: 0, 4: 1}
                if p not in pairs:
                    return
                u = 5 * pairs[p]
                pool.wait_ge(prob_free, count(ps.att, NU * GROUPS, NU * g + u + 5))
                pool.sem_inc(pool_passed, 1)
                blocks = probs[:, u:u + 5, :].rearrange("p u (k c) -> p (u k) c", c=P)
                for first, step_, n in ((0, 4, 5), (7, 3, 2), (19, 1, 1)):
                    view = blocks[:, first:first + step_ * (n - 1) + 1:step_, :]
                    pool.affine_select(out=view, in_=view, compare_op=ALU.is_ge, fill=0.0, base=0,
                                       pattern=[[0, n], [1, P]], channel_multiplier=-1).then_inc(selected, 1)

            def values(ps, g):
                pool.wait_ge(o_hi_done, count(ps.att, GROUPS, g + 1))
                pool.tensor_tensor(ot_lo[:, g, :], o_sb[:], ot_hi[:, g, :], ALU.subtract).then_inc(o_lo_done, 1)

            def lin(ps, c):
                m = P if c < HC - 1 else HLAST
                pool.wait_ge(g_hi_done, count(ps.ffn, HC, c + 1))
                pool.tensor_tensor(g_lo[0:m, c, :], g32[c % 2][0:m, :], g_hi[0:m, c, :],
                                   ALU.subtract).then_inc(g_lo_done, 1)

            def weight_sum(m):
                pool.wait_ge(abs_summed, PARTS * (WEIGHTS.index(m) + 1))
                all_reduce(abs_part_all[m], abs_part[m], RADD, PARTS)

            def run(ps):
                for step in ps.steps:
                    if step[0] == "probs":
                        select(ps, step[1], step[2])
                    elif step[0] == "values":
                        values(ps, step[1])
                    elif step[0] == "lin":
                        lin(ps, step[1])
                    elif step[0] == "stats_x":
                        power("x", ps.att + 1, step[1])
                    elif step[0] == "stats_y":
                        power("y", ps.att, step[1])
                    elif step[0] == "weight_sum" and step[2] == PARTS - 1:
                        weight_sum(step[1])

            passes(pool, run)

        @block.scalar
        def _(act):
            def weight_split():
                for c in range(KC):
                    if c == 0:
                        act.wait_ge(setup, 2)
                    act.activation(wqkv_hi[:, c, :], wqkv_raw[:, c, :], ACT.Copy,
                                   scale=scalar(w_scale)).then_inc(weights_hi, 1)

            def turned_high(ps, step, dst, i):
                s = ps.slot(step)
                act.wait_ge(work_full[s], ps.use(step))
                act.activation(dst[:, :, i * P:(i + 1) * P], work[s][:].rearrange("p (c s) -> p c s", c=KC),
                               ACT.Copy).then_inc(work_half, 1)

            def qk(ps, step):
                g = step[1]
                s, n = ps.slot(step), 2 * g + (step[0] == "k")
                if n or not ps.first:
                    act.wait_ge(hi_placed, count(ps.att, 2 * GROUPS, n))
                    act.wait_ge(lo_placed, count(ps.att, 2 * GROUPS, n))
                act.wait_ge(work_full[s], ps.use(step))
                act.activation(half_hi[:], work[s][:], ACT.Copy, scale=QK_SHRINK).then_inc(work_half, 1)

            def place(ps, step):
                g = step[1]
                act.wait_ge(work_half, ps.half(step))
                dst = (q_stack if step[0] == "q" else k_stack)[stack_of[g]]
                for h in range(HG):
                    last = act.activation(dst[0:HD, h, :], half_hi[HD * h:HD * (h + 1), :], ACT.Copy)
                last.then_inc(hi_placed, 1)

            def v(ps, step):
                i, s = step[1], ps.slot(step)
                act.wait_ge(work_full[s], ps.use(step))
                act.activation(v_sb[:, i, :], work[s][:], ACT.Copy, scale=V_SHRINK).then_inc(work_free[s], 1)

            def max_row(ps, step):
                s = ps.slot(step)
                act.wait_ge(work_full[s], ps.use(step))
                act.activation(max_hi[:], work[s][0:HG * ST, 0:P], ACT.Copy,
                               scale=1.0 / MAX_UNIT).then_inc(work_half, 1)

            def exp(ps, g, p):
                for u in (2 * p, 2 * p + 1):
                    act.wait_ge(prob_full, count(ps.att, NU * GROUPS, NU * g + u + 1))
                    act.activation(probs[:, u, :], prob_bank[u % 2][:], ACT.Exp,
                                   scale=scalar(exp_scale)).then_inc(prob_free, 1)

            def values(ps, g):
                act.wait_ge(o_ready, count(ps.att, GROUPS, g + 1))
                act.activation(ot_hi[:, g, :], o_sb[:], ACT.Copy).then_inc(o_hi_done, 1)

            def gate(ps, step):
                c, s = step[1], ps.slot(step)
                m = P if c < HC - 1 else HLAST
                act.wait_ge(work_full[s], ps.use(step))
                if c:
                    use = ("lin", c - 1)
                    act.wait_ge(work_free[ps.slot(use)], ps.use(use))
                act.activation(sig[0:m, :], work[s][0:m, :], ACT.Tanh,
                               scale=scalars[0:m, tanh_scale:tanh_scale + 1]).then_inc(tanh_done, 1)

            def lin(ps, c):
                m, use = P if c < HC - 1 else HLAST, ("lin", c)
                act.wait_ge(work_free[ps.slot(use)], ps.use(use))
                act.activation(g_hi[0:m, c, :], g32[c % 2][0:m, :], ACT.Copy).then_inc(g_hi_done, 1)

            def weight_sum(m, j):
                n = WEIGHTS.index(m)
                loads = 2 * (n + 1) - (m == "w2") if j == PARTS - 1 else n + 1
                act.wait_ge(raw_loaded[j], 16 * loads)
                src = raw_part(m, j)
                if PARTS * n + j:
                    act.wait_ge(abs_summed, PARTS * n + j)
                act.activation(magnitudes[:, 0:src.shape[1]], src, ACT.Abs,
                               accum_out=scalar(abs_part[m] + j)).then_inc(abs_summed, 1)

            def weight_ternary(ps, m, c):
                act.wait_ge(rounded, HC * WEIGHTS.index(m) + c + 1)
                if c == 0 and m != WEIGHTS[0]:
                    last = ("weight_turn", WEIGHTS[WEIGHTS.index(m) - 1], HC - 1)
                    act.wait_ge(work_full[ps.slot(last)], ps.use(last))
                src, dst = chunk_views(m, c)
                act.activation(dst, src, ACT.Sign, bias=scalar(neg_round)).then_inc(ternary_done, 1)

            def run(ps):
                for step in ps.steps:
                    if step[0] in ("xt", "xt_next"):
                        turned_high(ps, step, xt_hi, step[1])
                    elif step[0] == "weight_split":
                        weight_split()
                    elif step[0] == "wo_split":
                        act.wait_ge(setup, 5)
                        act.activation(wo_hi[:], wo_raw, ACT.Copy, scale=scalar(wo_scale)).then_inc(weights_hi, 1)
                    elif step[0] == "yt":
                        turned_high(ps, step, yt_hi, step[1])
                    elif step[0] in ("q", "k"):
                        qk(ps, step)
                    elif step[0] == "place":
                        place(ps, step[1:])
                    elif step[0] == "v":
                        v(ps, step)
                    elif step[0] == "max_row":
                        max_row(ps, step)
                    elif step[0] == "probs":
                        exp(ps, step[1], step[2])
                    elif step[0] == "values":
                        values(ps, step[1])
                    elif step[0] == "gate":
                        gate(ps, step)
                    elif step[0] == "lin":
                        lin(ps, step[1])
                    elif step[0] == "weight_sum":
                        weight_sum(step[1], step[2])
                    elif step[0] == "weight_ternary":
                        weight_ternary(ps, step[1], step[2])

            passes(act, run)

        @block.vector
        def _(dve):
            steps_done = [0]

            def scalar_step(ins):
                steps_done[0] += 1
                ins.then_inc(setup, 1)
                dve.wait_ge(setup, steps_done[0])

            def statistics(n, b, src, i):
                dve.bn_stats(stats[n][:, i, :], src[:, i, :]).then_inc(stats_done[n], 1)
                dve.wait_ge(stats_done[n], count(b, ST, i + 1))
                dve.sem_inc(dve_passed, 1)
                dve.bn_aggr(mean_var[n][:, i, :], stats[n][:, i, :]).then_inc(aggr_done[n], 1)
                dve.wait_ge(aggr_done[n], count(b, ST, i + 1))
                dve.tensor_scalar(var_eps[n][:, i:i + 1], mean_var[n][:, i, 1:2], EPS, NORM_SCALE ** -2,
                                  ALU.add, ALU.mult).then_inc(var_done[n], 1)

            def norm(n, b, src, dst, i):
                dve.wait_ge(rstd_done[n], count(b, ST, i + 1))
                dve.tensor_scalar(dst[:, i, :], src[:, i, :], mean_var[n][:, i, 0:1], rstd[n][:, i:i + 1],
                                  ALU.subtract, ALU.mult).then_inc(norm_done[n], 1)

            dve.memset(scalar(neg_round), -ROUND).then_inc(consts_done, 1)
            for i in range(ST):
                dve.wait_ge(x_first_loaded[i], 16)
                statistics("x", 0, xn, i)
            for i in range(ST):
                norm("x", 0, xn, xn, i)

            def unit_rows(i):
                dve.memset(k_stack[i][3 * HD:P, :, :], MAX_UNIT).then_inc(unit_rows_set, 1)

            def part_max(c):
                dve.wait_ge(wqkv_loaded[c], 16)
                dve.tensor_reduce(scalar(wmax_part + c), wqkv_raw[:, c, :], AX_X, ALU.max,
                                  apply_absolute_value=True).then_inc(part_max_done, 1)

            def weight_split():
                dve.wait_ge(part_max_done, KC)
                dve.tensor_reduce(scalar(wmax_all), scalar(wmax_part, KC), AX_X, ALU.max).then_inc(wmax_done, 1)
                dve.wait_ge(reduced, 1)
                scalar_step(dve.tensor_scalar(scalar(tmp), scalar(wmax_all), 1e-30, 1.0 / WEIGHT_TOP, ALU.max, ALU.mult))
                scalar_step(dve.reciprocal(scalar(w_scale), scalar(tmp)))
                shrink = NORM_SCALE * QK_SHRINK
                scalar_step(dve.tensor_scalar(scalar(exp_scale), scalar(tmp), scalar(tmp), HD ** -0.5 / shrink ** 2,
                                              ALU.mult, ALU.mult))
                dve.wait_ge(consts_done, 6)
                dve.tensor_scalar(mask_rows[:], ident[:], -MASK, None, ALU.mult).then_inc(mask_scaled, 1)
                for c in range(KC):
                    dve.wait_ge(weights_hi, c + 1)
                    dve.scalar_tensor_tensor(wqkv_lo[:, c, :], wqkv_raw[:, c, :], scalar(w_scale), wqkv_hi[:, c, :],
                                             ALU.mult, ALU.subtract).then_inc(weights_split, 1)

            def wo_max():
                dve.wait_ge(wo_loaded, 16)
                dve.tensor_reduce(scalar(womax_all), wo_raw.rearrange("p c n -> p (c n)"), AX_X, ALU.max,
                                  apply_absolute_value=True).then_inc(wmax_done, 1)
                dve.wait_ge(reduced, 2)
                scalar_step(dve.tensor_scalar(scalar(womax_all), scalar(womax_all), 1e-30, 1.0 / WEIGHT_TOP, ALU.max, ALU.mult))
                scalar_step(dve.reciprocal(scalar(wo_scale), scalar(womax_all)))
                scalar_step(dve.tensor_scalar(scalar(project_scale), scalar(womax_all), scalar(tmp),
                                              1.0 / (NORM_SCALE * V_SHRINK), ALU.mult, ALU.mult))

            def wo_split():
                dve.wait_ge(weights_hi, KC + 1)
                dve.scalar_tensor_tensor(wo_lo[:], wo_raw, scalar(wo_scale), wo_hi[:],
                                         ALU.mult, ALU.subtract).then_inc(weights_split, 1)

            def turned_low(ps, step, hi, lo, i):
                s = ps.slot(step)
                cols = slice(i * P, (i + 1) * P)
                dve.wait_ge(work_half, ps.half(step))
                dve.tensor_tensor(lo[:, :, cols], work[s][:].rearrange("p (c s) -> p c s", c=KC), hi[:, :, cols],
                                  ALU.subtract).then_inc(work_free[s], 1)

            def place(ps, step):
                g, s = step[1], ps.slot(step)
                dst, lo_row = (q_stack, HD) if step[0] == "q" else (k_stack, 2 * HD)
                dst = dst[stack_of[g]]
                dve.wait_ge(work_half, ps.half(step))
                dve.scalar_tensor_tensor(half_lo[:], work[s][:], QK_SHRINK, half_hi[:],
                                         ALU.mult, ALU.subtract).then_inc(work_free[s], 1)
                if g == GROUPS - 1:
                    dve.wait_ge(prob_full, count(ps.att, NU * GROUPS, NU))
                elif not ps.first:
                    dve.wait_ge(prob_full, count(ps.att, NU * GROUPS, 0))
                dve.wait_ge(work_free[s], ps.use(step))
                for h in range(HG):
                    last = dve.tensor_copy(dst[lo_row:lo_row + HD, h, :], half_lo[HD * h:HD * (h + 1), :])
                last.then_inc(lo_placed, 1)

            def max_row(ps, step):
                s = ps.slot(step)
                dve.wait_ge(work_half, ps.half(step))
                dve.scalar_tensor_tensor(max_lo[:], work[s][0:HG * ST, 0:P], 1.0 / MAX_UNIT, max_hi[:],
                                         ALU.mult, ALU.subtract).then_inc(work_free[s], 1)

            def maxima(ps, g, p):
                for u in (2 * p, 2 * p + 1):
                    dve.wait_ge(score_full, count(ps.att, NU * GROUPS, NU * g + u + 1))
                    dve.tensor_reduce(block_max[:, u, :], score_bank[u % 2][:].rearrange("p (k c) -> p k c", c=P),
                                      AX_X, ALU.max).then_inc(score_free, 1)
                if p < PIECES - 1:
                    return
                dve.wait_ge(score_free, count(ps.att, NU * GROUPS, NU * (g + 1)))
                bm = block_max[:].rearrange("p (a r) k -> p a r k", a=2)
                nm = neg_max[:].rearrange("p (a h) t -> p a h t", a=2)
                dve.tensor_reduce(nm[:, :, :, 3], bm[:, :, 0:4:3, :], AX_X, ALU.max, negate=True).then_inc(max_ready, 1)
                dve.tensor_reduce(nm[:, :, :, 2], bm[:, :, 1:5:3, 0:3], AX_X, ALU.max, negate=True).then_inc(max_ready, 1)
                dve.tensor_reduce(nm[:, :, :, 1], bm[:, :, 2, :].rearrange("p a (h k) -> p a h k", h=2),
                                  AX_X, ALU.max, negate=True).then_inc(max_ready, 1)
                dve.tensor_scalar(nm[:, :, :, 0], bm[:, :, 1:5:3, 3], -1.0, None, ALU.mult).then_inc(max_ready, 1)

            def values(ps, g):
                dve.wait_ge(sums_full, count(ps.att, GROUPS, g + 1))
                dve.reciprocal(inv_sum[:], sum_bank[:]).then_inc(inv_done, 1)
                dve.wait_ge(inv_done, count(ps.att, GROUPS, g + 1))
                dve.wait_ge(values_full, count(ps.att, GROUPS, g + 1))
                if g or not ps.first:
                    dve.wait_ge(o_lo_done, count(ps.att, GROUPS, g))
                dve.tensor_tensor(o_sb[:], o_bank[:], inv_sum[:], ALU.mult).then_inc(o_ready, 1)

            def project(ps, step):
                i, s = step[1], ps.slot(step)
                dve.wait_ge(work_full[s], ps.use(step))
                dve.wait_ge(res_loaded[i], count(ps.att, 16, 16))
                dve.scalar_tensor_tensor(x_res[:, i, :], work[s][:], scalar(project_scale), x_res[:, i, :],
                                         ALU.mult, ALU.add).then_inc(work_free[s], 1)

            def gate(ps, step):
                c, s = step[1], ps.slot(step)
                m = P if c < HC - 1 else HLAST
                dve.wait_ge(tanh_done, count(ps.ffn, HC, c + 1))
                dve.scalar_tensor_tensor(sig[0:m, :], sig[0:m, :], 1.0, work[s][0:m, :],
                                         ALU.add, ALU.mult).then_inc(work_free[s], 1)

            def lin(ps, step):
                c, s = step[1], ps.slot(step)
                m = P if c < HC - 1 else HLAST
                dve.wait_ge(work_full[s], ps.use(step))
                before = ("gate", c)
                dve.wait_ge(work_free[ps.slot(before)], ps.use(before))
                if c >= 2:
                    dve.wait_ge(g_lo_done, count(ps.ffn, HC, c - 1))
                dve.scalar_tensor_tensor(g32[c % 2][0:m, :], sig[0:m, :], G_SHRINK, work[s][0:m, :],
                                         ALU.mult, ALU.mult).then_inc(work_free[s], 1)

            def down(ps, step):
                i, s = step[1], ps.slot(step)
                dve.wait_ge(work_full[s], ps.use(step))
                dve.scalar_tensor_tensor(x_res[:, i, :], work[s][:], scalar(down_scale), x_res[:, i, :],
                                         ALU.mult, ALU.add).then_inc(work_free[s], 1)

            def weight_load(m, j):
                if m == "w1" and j == 0:
                    dve.wait_ge(weights_split, KC)
                    dve.memset(raw_rows[:, HC - 1, :], 0.0).then_inc(pad_zeroed, 1)

            def weight_scales(m):
                dve.wait_ge(reduced, 3 + WEIGHTS.index(m))
                scalar_step(dve.tensor_reduce(scalar(abs_all[m]), scalar(abs_part_all[m], PARTS), AX_X, ALU.add))
                scalar_step(dve.tensor_scalar(scalar(half_s[m]), scalar(abs_all[m]), 0.5 / (HIDDEN * D), None, ALU.mult))
                scalar_step(dve.tensor_scalar(scalar(inv_s[m]), scalar(half_s[m]), 2.0, None, ALU.mult))
                scalar_step(dve.reciprocal(scalar(inv_s[m]), scalar(inv_s[m])))
                if m == "w1":
                    scalar_step(dve.tensor_scalar(scalar(tanh_scale), scalar(half_s[m]), 1.0 / NORM_SCALE, None, ALU.mult))
                if m == "w2":
                    k = 8.0 / (2.0 * NORM_SCALE ** 2 * G_SHRINK)
                    scalar_step(dve.tensor_scalar(scalar(down_scale), scalar(half_s["w1"]), scalar(half_s["w3"]), k,
                                                  ALU.mult, ALU.mult))
                    scalar_step(dve.tensor_scalar(scalar(down_scale), scalar(down_scale), scalar(half_s[m]), None, ALU.mult))

            def weight_turn(ps, step):
                _, m, c = step
                s, cols = ps.slot(step), P if c < HC - 1 else HLAST
                src = work[s][:, 0:256].bitcast(F16).rearrange("p (k c) -> p k c", k=KC)
                dve.wait_ge(work_full[s], ps.use(step))
                if m == "w2":
                    dst = t_down[0:cols, c, :].rearrange("p (k c) -> p k c", k=KC)
                    dve.tensor_copy(dst, src[0:cols, :, :]).then_inc(work_free[s], 1)
                else:
                    dve.tensor_copy(t_up[m][:, :, c * P:c * P + cols], src[:, :, 0:cols]).then_inc(work_free[s], 1)

            def weight_round(m, c):
                if c == 0:
                    weight_scales(m)
                rows = HLAST if m != "w2" and c == HC - 1 else P
                src = chunk_views(m, c)[0][0:rows]
                dve.tensor_scalar(src, src, scalars[0:rows, inv_s[m]:inv_s[m] + 1], ROUND, ALU.mult, ALU.add).then_inc(rounded, 1)

            def run(ps):
                for step in ps.steps:
                    if step[0] in ("xt", "xt_next"):
                        turned_low(ps, step, xt_hi, xt_lo, step[1])
                        if step[0] == "xt":
                            part_max(step[1])
                    elif step[0] == "weight_split":
                        weight_split()
                    elif step[0] == "unit_rows":
                        unit_rows(step[1])
                    elif step[0] == "wo_split":
                        wo_split()
                    elif step[0] == "wo_max":
                        wo_max()
                    elif step[0] == "yt":
                        turned_low(ps, step, yt_hi, yt_lo, step[1])
                    elif step[0] == "place":
                        place(ps, step[1:])
                    elif step[0] == "max_row":
                        max_row(ps, step)
                    elif step[0] == "scores":
                        maxima(ps, step[1], step[2])
                    elif step[0] == "values":
                        values(ps, step[1])
                    elif step[0] == "project":
                        project(ps, step)
                    elif step[0] == "stats_x":
                        if step[1] == 0:
                            dve.wait_ge(x_loaded, count(ps.att, 16, 16))
                        statistics("x", ps.att + 1, xn, step[1])
                    elif step[0] == "norm_x":
                        norm("x", ps.att + 1, xn, xn, step[1])
                    elif step[0] == "stats_y":
                        use = ("project", step[1])
                        dve.wait_ge(work_free[ps.slot(use)], ps.use(use))
                        dve.sem_inc(dve_passed, 1)
                        statistics("y", ps.att, x_res, step[1])
                    elif step[0] == "norm_y":
                        norm("y", ps.ffn, x_res, yn, step[1])
                    elif step[0] == "gate":
                        gate(ps, step)
                    elif step[0] == "lin":
                        lin(ps, step)
                    elif step[0] == "down":
                        down(ps, step)
                    elif step[0] == "weight_load":
                        weight_load(step[1], step[2])
                    elif step[0] == "weight_turn":
                        weight_turn(ps, step)
                    elif step[0] == "weight_round":
                        weight_round(step[1], step[2])

            passes(dve, run)

        @block.tensor
        def _(pe):
            pe.wait_ge(consts_done, 6)

            def open_work(ps, step):
                s, k = ps.slot(step), ps.use(step) - 1
                if not (isinstance(k, int) and k == 0):
                    pe.wait_ge(work_free[s], k)
                return s

            def evacuated(ps, step):
                pe.wait_ge(work_free[ps.slot(step)], ps.use(step))

            def products(bank, terms):
                for n, (lhs, rhs) in enumerate(terms):
                    last = pe.matmul(bank, lhs, rhs, start=(n == 0), stop=(n == len(terms) - 1))
                return last

            def turn(ps, step, src, ready, b):
                i = step[1]
                s = open_work(ps, step)
                pe.wait_ge(ready, count(b, ST, i + 1))
                for c in range(KC):
                    last = pe.transpose(work[s][:, c * P:(c + 1) * P], src[:, i, c * P:(c + 1) * P], ident[:])
                last.then_inc(work_full[s], 1)

            def split_terms(a_hi, a_lo, b_hi, b_lo):
                return [(a_hi, b_hi), (a_hi, b_lo), (a_lo, b_hi)]

            def qk(ps, step):
                g = step[1]
                s = open_work(ps, step)
                if step == ("q", 0):
                    for i in (ST - 2, ST - 1):
                        if ps.first:
                            evacuated(ps, ("xt", i))
                        else:
                            bank, value = ps.previous(("xt_next", i))
                            pe.wait_ge(work_free[bank], value)
                cols = slice((step[0] == "k") * D + g * P, (step[0] == "k") * D + (g + 1) * P)
                for c in range(KC):
                    if ps.first and step == ("q", 0):
                        pe.wait_ge(weights_split, c + 1)
                    for n, (w, xx) in enumerate(split_terms(wqkv_hi, wqkv_lo, xt_hi, xt_lo)):
                        last = pe.matmul(work[s][:], w[:, c, cols], xx[:, c, :],
                                         start=(c == 0 and n == 0), stop=(c == KC - 1 and n == 2))
                last.then_inc(work_full[s], 1)

            def v(ps, step):
                i = step[1]
                s = open_work(ps, step)
                rows = slice(i * P, (i + 1) * P)
                terms = []
                for c in range(KC):
                    terms += [(a[:, c, rows], w[:, c, 2 * D:3 * D])
                              for a, w in split_terms(xt_hi, xt_lo, wqkv_hi, wqkv_lo)]
                products(work[s][:], terms).then_inc(work_full[s], 1)

            def scores(ps, g, p):
                if p == 0:
                    pe.wait_ge(stacked[g], count(ps.att, 32, 32))
                    if g == 0 and ps.first:
                        pe.wait_ge(mask_scaled, 1)
                q, k = q_stack[stack_of[g]], k_stack[stack_of[g]]
                for u in (2 * p, 2 * p + 1):
                    if u >= 2 or g or not ps.first:
                        pe.wait_ge(score_free, count(ps.att, NU * GROUPS, NU * g + u - 1))
                    bank = score_bank[u % 2]
                    for h, tile, off, n in UNITS[u]:
                        pe.matmul(bank[:, off:off + n], q[0:3 * HD, h, tile * P:(tile + 1) * P],
                                  k[0:3 * HD, h, 0:n], start=True, stop=False)
                        last = pe.matmul(bank[:, off + n - P:off + n], mask_rows[:], mask_cols[:],
                                         start=False, stop=True)
                    last.then_inc(score_full, 1)

            def max_row(ps, step):
                g = step[1]
                s = open_work(ps, step)
                pe.wait_ge(max_ready, count(ps.att, 4 * GROUPS, 4 * g + 4))
                pe.transpose(work[s][0:HG * ST, 0:P], neg_max[:].rearrange("p h t -> p (h t)"),
                             ident[:]).then_inc(work_full[s], 1)

            def probs_(ps, g, p):
                if p == 0:
                    if ps.first and g < len(k_stack):
                        pe.wait_ge(unit_rows_set, g + 1)
                    pe.wait_ge(max_placed[g], count(ps.att, 32, 32))
                q, k = q_stack[stack_of[g]], k_stack[stack_of[g]]
                rows = 3 * HD + 2
                for u in (2 * p, 2 * p + 1):
                    if u >= 2 or g or not ps.first:
                        pe.wait_ge(prob_free, count(ps.att, NU * GROUPS, NU * g + u - 1))
                    bank = prob_bank[u % 2]
                    for h, tile, off, n in UNITS[u]:
                        kt = ST - 1 - tile
                        last = pe.matmul(bank[:, off:off + n], k[0:rows, h, kt * P:(kt + 1) * P],
                                         q[0:rows, h, S - n:S], start=True, stop=True)
                    last.then_inc(prob_full, 1)

            def values(ps, g):
                if g == 0:
                    evacuated(ps, ("v", ST - 2))
                    evacuated(ps, ("v", ST - 1))
                pe.wait_ge(selected, count(ps.att, SELECTS * GROUPS, SELECTS * (g + 1)))
                if g or not ps.first:
                    pe.wait_ge(o_ready, count(ps.att, GROUPS, g))
                for bank, full in ((sum_bank, sums_full), (o_bank, values_full)):
                    for kt in range(ST):
                        for h in range(HG):
                            u, off, n = [(u, off, n) for u in range(NU) for hh, tile, off, n in UNITS[u]
                                         if (hh, tile) == (h, ST - 1 - kt)][0]
                            col = (g * HG + h) * HD
                            lhs = ones[:] if bank is sum_bank else v_sb[:, kt, col:col + HD]
                            last = pe.matmul(bank[HD * h:HD * (h + 1), S - n:S], lhs, probs[:, u, off:off + n],
                                             start=(kt == 0), stop=(kt == ST - 1), skip_group_check=True)
                    last.then_inc(full, 1)

            def project(ps, step):
                i = step[1]
                s = open_work(ps, step)
                if i == 0:
                    pe.wait_ge(o_lo_done, count(ps.att, GROUPS, GROUPS))
                    if ps.first:
                        pe.wait_ge(weights_split, KC + 1)
                rows = slice(i * P, (i + 1) * P)
                terms = []
                for c in range(GROUPS):
                    terms += [(a[:, c, rows], w[:, c, :]) for a, w in split_terms(ot_hi, ot_lo, wo_hi, wo_lo)]
                products(work[s][:], terms).then_inc(work_full[s], 1)

            def up(ps, step):
                c = step[1]
                m = P if c < HC - 1 else HLAST
                s = open_work(ps, step)
                if step == ("gate", 0):
                    evacuated(ps, ("yt", ST - 1))
                    evacuated(ps, ("yt", ST - 2))
                w = t_up["w1" if step[0] == "gate" else "w3"]
                terms = [(w[:, k, c * P:c * P + m], y[:, k, :]) for k in range(KC) for y in (yt_hi, yt_lo)]
                products(work[s][0:m, :], terms).then_inc(work_full[s], 1)

            def down(ps, step):
                i = step[1]
                s = open_work(ps, step)
                for c in range(HC):
                    m = P if c < HC - 1 else HLAST
                    if i == 0:
                        pe.wait_ge(g_lo_done, count(ps.ffn, HC, c + 1))
                    for g in (g_hi, g_lo):
                        last = pe.matmul(work[s][:], g[0:m, c, i * P:(i + 1) * P], t_down[0:m, c, :],
                                         start=(c == 0 and g is g_hi), stop=(c == HC - 1 and g is g_lo))
                last.then_inc(work_full[s], 1)

            def weight_turn(ps, step):
                _, m, c = step
                s = open_work(ps, step)
                cols = P if c < HC - 1 else HLAST
                bank = work[s][:, 0:256].bitcast(F16)
                pe.wait_ge(ternary_done, HC * WEIGHTS.index(m) + c + 1)
                for k in range(KC):
                    if m == "w2":
                        src = nat[:, 0:ST * HIDDEN].rearrange("p (k n) -> p k n", k=ST)[:, k, c * P:c * P + cols]
                        last = pe.transpose(bank[0:cols, k * P:(k + 1) * P], src, ident16[:])
                    else:
                        src = nat[:, c * D + k * P:c * D + (k + 1) * P]
                        last = pe.transpose(bank[:, k * P:(k + 1) * P], src, ident16[:])
                last.then_inc(work_full[s], 1)

            def run(ps):
                for step in ps.steps:
                    if step[0] == "xt":
                        turn(ps, step, xn, norm_done["x"], 0)
                    elif step[0] == "xt_next":
                        turn(ps, step, xn, norm_done["x"], ps.att + 1)
                    elif step[0] == "yt":
                        turn(ps, step, yn, norm_done["y"], ps.ffn)
                    elif step[0] in ("q", "k"):
                        qk(ps, step)
                    elif step[0] == "v":
                        v(ps, step)
                    elif step[0] == "scores":
                        scores(ps, step[1], step[2])
                    elif step[0] == "max_row":
                        max_row(ps, step)
                    elif step[0] == "probs":
                        probs_(ps, step[1], step[2])
                    elif step[0] == "values":
                        values(ps, step[1])
                    elif step[0] == "project":
                        project(ps, step)
                    elif step[0] in ("gate", "lin"):
                        up(ps, step)
                    elif step[0] == "down":
                        down(ps, step)
                    elif step[0] == "weight_turn":
                        weight_turn(ps, step)

            passes(pe, run)


_INS = ["L0_attn_x", "L0_attn_Wqkv", "L0_attn_Wo", "L0_ffn_w1", "L0_ffn_w3", "L0_ffn_w2"]


def kernel(**inputs):
    import numpy as np
    import concourse.bacc as bacc
    from concourse.bass_utils import run_bass_kernel_spmd

    nc = bacc.Bacc("TRN2", target_bir_lowering=False, num_devices=1)
    arrays, args = {}, []
    for name in _INS:
        a = np.ascontiguousarray(inputs[name])
        arrays[f"in_{name}"] = a
        args.append(nc.dram_tensor(f"in_{name}", a.shape, mybir.dt.from_np(a.dtype), kind="ExternalInput").ap())
    out = nc.dram_tensor("out_y", (BATCHES, S, D), F32, kind="ExternalOutput").ap()
    build(nc, *args, out)
    r = run_bass_kernel_spmd(nc, [arrays], core_ids=[0])
    return r.results[0]["out_y"]
```
